# Optimizing a Trainium2 kernel written in Bass

```python
import numpy as np
import jax
import jax.numpy as jnp

def _softmax(x, axis=-1):
    return jax.nn.softmax(x, axis=axis)

def _gelu(x):
    return jax.nn.gelu(x, approximate=True)

def _silu(x):
    return jax.nn.silu(x)

def _sigmoid(x):
    return jax.nn.sigmoid(x)

def _layernorm(x, axis=-1, eps=1e-05):
    m = jnp.mean(x, axis=axis, keepdims=True)
    v = jnp.var(x, axis=axis, keepdims=True)
    return (x - m) / jnp.sqrt(v + eps)

def _scatter_add(tgt, idx, src, axis=0):
    return tgt.at[idx].add(src)

def _segment_sum(src, seg, n):
    return jax.ops.segment_sum(src, seg, n)
kernel_name = 'mk_dlrm_tower_d1_rec_r8_313ef2'

def setup_inputs(seed: int=0):
    np.random.seed(seed)
    _w = jnp.asarray

    def _rec_inputs():
        import jax
        import jax.numpy as jnp
        _tk = jax.random.key(seed)
        ids = jnp.stack([jax.random.randint(jax.random.fold_in(_tk, 200 + f), (512,), 0, v, jnp.int32) for f, v in enumerate([1000, 125000, 1000, 1250, 1000, 1250, 1000, 12500, 12500, 1250, 1000, 12500, 1000, 12500, 1250, 1000, 1000, 1000, 1000, 1000, 12500, 1000, 12500, 1000, 1250, 1250])], axis=1)
        tbl_0 = 0.05 * jax.random.normal(jax.random.fold_in(_tk, 500 + 0), (1000, 128), jnp.float32)
        tbl_1 = 0.05 * jax.random.normal(jax.random.fold_in(_tk, 500 + 1), (125000, 128), jnp.float32)
        tbl_2 = 0.05 * jax.random.normal(jax.random.fold_in(_tk, 500 + 2), (1000, 128), jnp.float32)
        tbl_3 = 0.05 * jax.random.normal(jax.random.fold_in(_tk, 500 + 3), (1250, 128), jnp.float32)
        tbl_4 = 0.05 * jax.random.normal(jax.random.fold_in(_tk, 500 + 4), (1000, 128), jnp.float32)
        tbl_5 = 0.05 * jax.random.normal(jax.random.fold_in(_tk, 500 + 5), (1250, 128), jnp.float32)
        tbl_6 = 0.05 * jax.random.normal(jax.random.fold_in(_tk, 500 + 6), (1000, 128), jnp.float32)
        tbl_7 = 0.05 * jax.random.normal(jax.random.fold_in(_tk, 500 + 7), (12500, 128), jnp.float32)
        tbl_8 = 0.05 * jax.random.normal(jax.random.fold_in(_tk, 500 + 8), (12500, 128), jnp.float32)
        tbl_9 = 0.05 * jax.random.normal(jax.random.fold_in(_tk, 500 + 9), (1250, 128), jnp.float32)
        tbl_10 = 0.05 * jax.random.normal(jax.random.fold_in(_tk, 500 + 10), (1000, 128), jnp.float32)
        tbl_11 = 0.05 * jax.random.normal(jax.random.fold_in(_tk, 500 + 11), (12500, 128), jnp.float32)
        tbl_12 = 0.05 * jax.random.normal(jax.random.fold_in(_tk, 500 + 12), (1000, 128), jnp.float32)
        tbl_13 = 0.05 * jax.random.normal(jax.random.fold_in(_tk, 500 + 13), (12500, 128), jnp.float32)
        tbl_14 = 0.05 * jax.random.normal(jax.random.fold_in(_tk, 500 + 14), (1250, 128), jnp.float32)
        tbl_15 = 0.05 * jax.random.normal(jax.random.fold_in(_tk, 500 + 15), (1000, 128), jnp.float32)
        tbl_16 = 0.05 * jax.random.normal(jax.random.fold_in(_tk, 500 + 16), (1000, 128), jnp.float32)
        tbl_17 = 0.05 * jax.random.normal(jax.random.fold_in(_tk, 500 + 17), (1000, 128), jnp.float32)
        tbl_18 = 0.05 * jax.random.normal(jax.random.fold_in(_tk, 500 + 18), (1000, 128), jnp.float32)
        tbl_19 = 0.05 * jax.random.normal(jax.random.fold_in(_tk, 500 + 19), (1000, 128), jnp.float32)
        tbl_20 = 0.05 * jax.random.normal(jax.random.fold_in(_tk, 500 + 20), (12500, 128), jnp.float32)
        tbl_21 = 0.05 * jax.random.normal(jax.random.fold_in(_tk, 500 + 21), (1000, 128), jnp.float32)
        tbl_22 = 0.05 * jax.random.normal(jax.random.fold_in(_tk, 500 + 22), (12500, 128), jnp.float32)
        tbl_23 = 0.05 * jax.random.normal(jax.random.fold_in(_tk, 500 + 23), (1000, 128), jnp.float32)
        tbl_24 = 0.05 * jax.random.normal(jax.random.fold_in(_tk, 500 + 24), (1250, 128), jnp.float32)
        tbl_25 = 0.05 * jax.random.normal(jax.random.fold_in(_tk, 500 + 25), (1250, 128), jnp.float32)
        _rk = jax.random.fold_in(_tk, 7)
        r_dense_features = -0.000520686 + 1.00062 * jax.random.normal(jax.random.fold_in(_rk, 101), (512, 128), jnp.float32)
        W_top1 = 0.0405887 * jax.random.normal(jax.random.fold_in(_tk, 801), (607, 512), jnp.float32)
        W_top2 = 0.0441942 * jax.random.normal(jax.random.fold_in(_tk, 802), (512, 256), jnp.float32)
        W_top3 = 0.0625 * jax.random.normal(jax.random.fold_in(_tk, 803), (256, 1), jnp.float32)
        b_top1 = jnp.zeros((512,), jnp.float32)
        b_top2 = jnp.zeros((256,), jnp.float32)
        return (r_dense_features, ids, tbl_0, tbl_1, tbl_2, tbl_3, tbl_4, tbl_5, tbl_6, tbl_7, tbl_8, tbl_9, tbl_10, tbl_11, tbl_12, tbl_13, tbl_14, tbl_15, tbl_16, tbl_17, tbl_18, tbl_19, tbl_20, tbl_21, tbl_22, tbl_23, tbl_24, tbl_25, W_top1, b_top1, W_top2, b_top2, W_top3)
    r_dense_features, ids, tbl_0, tbl_1, tbl_2, tbl_3, tbl_4, tbl_5, tbl_6, tbl_7, tbl_8, tbl_9, tbl_10, tbl_11, tbl_12, tbl_13, tbl_14, tbl_15, tbl_16, tbl_17, tbl_18, tbl_19, tbl_20, tbl_21, tbl_22, tbl_23, tbl_24, tbl_25, W_top1, b_top1, W_top2, b_top2, W_top3 = _rec_inputs()

    def _L0_rec_setup():
        import jax, jax.numpy as jnp
        import numpy as np
        NUM_SPARSE = 26
        EMBED_DIM = 128
        BATCH = 2048
        key = jax.random.key(seed)
        k1, k2 = jax.random.split(key)
        dense_features = jax.random.normal(k1, (BATCH, EMBED_DIM), dtype=jnp.float32)
        sparse_features = jax.random.normal(k2, (BATCH, NUM_SPARSE, EMBED_DIM), dtype=jnp.float32)
        return {'dense_features': dense_features, 'sparse_features': sparse_features}
    _L0_rec_all = _L0_rec_setup()
    _L0_rec_in = {k: v for k, v in _L0_rec_all.items() if k in ()}
    del _L0_rec_all
    return {'r_dense_features': r_dense_features, 'ids': ids, 'tbl_0': tbl_0, 'tbl_1': tbl_1, 'tbl_2': tbl_2, 'tbl_3': tbl_3, 'tbl_4': tbl_4, 'tbl_5': tbl_5, 'tbl_6': tbl_6, 'tbl_7': tbl_7, 'tbl_8': tbl_8, 'tbl_9': tbl_9, 'tbl_10': tbl_10, 'tbl_11': tbl_11, 'tbl_12': tbl_12, 'tbl_13': tbl_13, 'tbl_14': tbl_14, 'tbl_15': tbl_15, 'tbl_16': tbl_16, 'tbl_17': tbl_17, 'tbl_18': tbl_18, 'tbl_19': tbl_19, 'tbl_20': tbl_20, 'tbl_21': tbl_21, 'tbl_22': tbl_22, 'tbl_23': tbl_23, 'tbl_24': tbl_24, 'tbl_25': tbl_25, 'W_top1': W_top1, 'b_top1': b_top1, 'W_top2': W_top2, 'b_top2': b_top2, 'W_top3': W_top3}

def reference(r_dense_features, ids, tbl_0, tbl_1, tbl_2, tbl_3, tbl_4, tbl_5, tbl_6, tbl_7, tbl_8, tbl_9, tbl_10, tbl_11, tbl_12, tbl_13, tbl_14, tbl_15, tbl_16, tbl_17, tbl_18, tbl_19, tbl_20, tbl_21, tbl_22, tbl_23, tbl_24, tbl_25, W_top1, b_top1, W_top2, b_top2, W_top3):
    import jax
    import jax.numpy as jnp

    def _L0_rec_ref(dense_features, sparse_features):
        import jax, jax.numpy as jnp
        import numpy as np
        NUM_SPARSE = 26
        EMBED_DIM = 128
        BATCH = 2048
        F = NUM_SPARSE + 1
        combined = jnp.concatenate([dense_features[:, None, :], sparse_features], axis=1)
        interactions = jnp.einsum('bfd,bgd->bfg', combined, combined)
        iu, ju = jnp.triu_indices(F, k=1)
        interactions_flat = interactions[:, iu, ju]
        return jnp.concatenate([dense_features, interactions_flat], axis=1)
    e = jnp.stack([tbl_0[ids[:, 0]], tbl_1[ids[:, 1]], tbl_2[ids[:, 2]], tbl_3[ids[:, 3]], tbl_4[ids[:, 4]], tbl_5[ids[:, 5]], tbl_6[ids[:, 6]], tbl_7[ids[:, 7]], tbl_8[ids[:, 8]], tbl_9[ids[:, 9]], tbl_10[ids[:, 10]], tbl_11[ids[:, 11]], tbl_12[ids[:, 12]], tbl_13[ids[:, 13]], tbl_14[ids[:, 14]], tbl_15[ids[:, 15]], tbl_16[ids[:, 16]], tbl_17[ids[:, 17]], tbl_18[ids[:, 18]], tbl_19[ids[:, 19]], tbl_20[ids[:, 20]], tbl_21[ids[:, 21]], tbl_22[ids[:, 22]], tbl_23[ids[:, 23]], tbl_24[ids[:, 24]], tbl_25[ids[:, 25]]], axis=1)
    z = _L0_rec_ref(r_dense_features, e)
    z = z.reshape(z.shape[0], -1)
    h = jnp.concatenate([z, r_dense_features], axis=1)
    h = jnp.maximum(h @ W_top1 + b_top1, 0.0)
    h = jnp.maximum(h @ W_top2 + b_top2, 0.0)
    y = h @ W_top3
    return y

_drawn_inputs = setup_inputs


def setup_inputs(seed=0):
    import zlib

    import numpy as np

    out = dict(_drawn_inputs(seed))
    spreads = {'b_top1': (0.0, 0.1), 'b_top2': (0.0, 0.1)}
    factors = {}
    for name, (base, spread) in spreads.items():
        noise = np.random.default_rng([zlib.crc32(name.encode()), seed]).standard_normal(out[name].shape)
        drawn = base * np.exp(spread * noise) if base else spread * noise
        out[name] = jnp.asarray(drawn.astype(out[name].dtype))
    for name, factor in factors.items():
        out[name] = (out[name] * factor).astype(out[name].dtype)
    return out
```

```python
import concourse.bass as bass
from concourse import mybir
from contextlib import ExitStack

P = 128
BATCH, D = 512, 128
TABLES = 26
TILES = BATCH // P
FEATURES = TABLES + 1
SLOTS = 32
H1, H2 = 512, 256

ONEHOT_TABLES = (0, 2, 4, 6, 10, 12)
GATHERED_TABLES = tuple(f for f in range(TABLES) if f not in ONEHOT_TABLES)
SLOT_TABLE = ONEHOT_TABLES + GATHERED_TABLES
N_ONEHOT, N_GATHERED = len(ONEHOT_TABLES), len(GATHERED_TABLES)
TABLE_ROWS = 1024
ROW_BLOCKS = TABLE_ROWS // P

TURN = 4
TURNS = -(-N_GATHERED // TURN)
COLUMNS = FEATURES - 1
LOW, HIGH = slice(0, 64), slice(64, 128)
QUADS = 4
GROUPS = P // QUADS // 2
K_TILES = -(-COLUMNS // QUADS)
SPLIT_RING = 2


def columns_of(j):
    return len(range(j, COLUMNS, QUADS))


def schedule():
    steps = [("dense",), ("ids", 0)]
    for i in range(N_ONEHOT):
        if i + 1 < N_ONEHOT:
            steps.append(("ids", i + 1))
        steps.append(("onehot", i))
    steps += [("turn", 0, q) for q in range(TURNS)]
    for t in range(TILES):
        ahead = [("turn", t + 1, q) for q in range(TURNS)] if t + 1 < TILES else []
        for own in (("gram", t, 0), ("gram", t, 1), ("layer1", t), ("layer2", t), ("layer3", t)):
            steps.append(own)
            if ahead:
                steps.append(ahead.pop(0))
        steps += ahead
    return steps


STEPS = schedule()
RING = [s for s in STEPS if s[0] in ("dense", "ids", "onehot", "turn")]


def drained_by(step):
    if step[0] == "turn" and step[2] % 2 == 1:
        return "vector"
    return "scalar"


def drains(step):
    upto = RING[: RING.index(step) + 1]
    return sum(drained_by(s) == drained_by(step) for s in upto)


def dlrm_tower(nc, dense, ids, ids_rows, tables, onehot_tables, w1_dense, w1_pairs, w2, w3, b1, b2,
               identity, row_numbers, row_pick, out):
    f32, f32r, f16, i32 = (mybir.dt.float32, mybir.dt.float32r, mybir.dt.float16, mybir.dt.int32)
    ALU = mybir.AluOpType
    ACT = mybir.ActivationFunctionType

    ctx = ExitStack()
    with ctx:
        def sb(name, shape, dt):
            return ctx.enter_context(nc.sbuf_tensor(name, shape, dt))

        def psum(name, shape):
            return ctx.enter_context(nc.psum_tensor(name, shape, f32))

        def sem(name):
            return ctx.enter_context(nc.semaphore(name))

        ids_sb = sb("ids_sb", [P, TILES, TABLES], i32)
        ids_int = sb("ids_int", [N_ONEHOT, BATCH], i32)
        ids_half = sb("ids_half", [N_ONEHOT, BATCH], f16)
        pick = sb("pick", [N_ONEHOT, N_ONEHOT, P], f16)
        ident = sb("ident", [P, P], f32)
        row_no = sb("row_no", [P, ROW_BLOCKS], f32)
        dense_sb = sb("dense_sb", [P, TILES, D], f32)
        rows = sb("rows", [P, TILES, N_GATHERED, D], f32)
        table_sb = sb("table_sb", [P, SPLIT_RING, ROW_BLOCKS, D], f32)
        table_hi = sb("table_hi", [P, SPLIT_RING, ROW_BLOCKS, D], f32r)
        table_lo = sb("table_lo", [P, SPLIT_RING, ROW_BLOCKS, D], f32r)
        ids_bc = sb("ids_bc", [P, 2, BATCH], f16)
        onehot = sb("onehot", [P, 2, ROW_BLOCKS, BATCH], f32r)
        eT = sb("eT", [P, BATCH, SLOTS], f32)
        denseT = sb("denseT", [P, TILES, QUADS, P // QUADS], f32)
        pairs = sb("pairs", [P, 2, K_TILES, QUADS, P // QUADS], f32)
        wd2 = sb("wd2", [P, 2, H1], f32)
        wd = sb("wd", [P, H1], f32)
        wp = sb("wp", [P, K_TILES, H1], f32)
        w2_sb = sb("w2_sb", [P, H1 // P, H2], f32)
        w3_sb = sb("w3_sb", [P, H2 // P], f32)
        b1_sb = sb("b1_sb", [P, H1 // P], f32)
        b2_sb = sb("b2_sb", [P, H2 // P], f32)
        h1 = sb("h1", [P, H1 // P, P], f32)
        h2 = sb("h2", [P, H2 // P, P], f32)
        y = sb("y", [1, BATCH], f32)

        ring = [psum(f"ring{n}", [P, 512]) for n in range(2)]
        gram = psum("gram", [P, GROUPS, P])
        h1_ps = psum("h1_ps", [P, H1 // P, P])
        h2_ps = psum("h2_ps", [P, 512])
        y_ps = h2_ps[0:1, H2:H2 + P]

        ids_landed = sem("ids_landed")
        id_rows_landed = sem("id_rows_landed")
        dense_landed = sem("dense_landed")
        table_landed = [sem(f"table_landed{n}") for n in range(SPLIT_RING)]
        wd_landed = sem("wd_landed")
        w1_landed = sem("w1_landed")
        mlp_landed = sem("mlp_landed")
        rows_landed = [[sem(f"rows_landed{t}_{q}") for q in range(TURNS)] for t in range(TILES)]
        out_written = sem("out_written")

        cleared = sem("cleared")
        ids_half_ready = sem("ids_half_ready")
        hi_ready = sem("hi_ready")
        lo_ready = sem("lo_ready")
        onehot_ready = sem("onehot_ready")
        wd_ready = sem("wd_ready")
        ring_filled = sem("ring_filled")
        drained = {"scalar": sem("drained_scalar"), "vector": sem("drained_vector")}
        dense_copied = sem("dense_copied")
        gram_filled = sem("gram_filled")
        pairs_scalar = sem("pairs_scalar")
        pairs_vector = sem("pairs_vector")
        h1_filled = sem("h1_filled")
        h1_scalar = sem("h1_scalar")
        h1_vector = sem("h1_vector")
        h2_filled = sem("h2_filled")
        h2_scalar = sem("h2_scalar")
        h2_vector = sem("h2_vector")
        y_filled = sem("y_filled")
        y_ready = sem("y_ready")

        block = ctx.enter_context(nc.Block())

        def tile(t):
            return slice(t * P, (t + 1) * P)

        def turned(q):
            return range(q * TURN, min((q + 1) * TURN, N_GATHERED))

        def drain_target(step):
            if step[0] == "dense":
                return eT[:, :, 0], BATCH
            if step[0] == "onehot":
                return eT[:, :, 1 + step[1]], BATCH
            _, t, q = step
            slot = 1 + N_ONEHOT + q * TURN
            n = len(turned(q))
            return eT[:, tile(t), slot:slot + n].rearrange("p b f -> p f b"), n * P

        def drain_source(step):
            bank = ring[RING.index(step) % 2]
            if step[0] == "turn":
                n = len(turned(step[2]))
                return bank[:, 0:n * P].rearrange("p (f b) -> p f b", f=n)
            return bank[:, 0:BATCH]

        def pairs_parts(t, half, s, j):
            n = columns_of(j)
            at = slice(half * GROUPS, (half + 1) * GROUPS)
            first = s * COLUMNS + j
            src = gram[32 * s:32 * s + 32, :, first:first + QUADS * (n - 1) + 1:QUADS]
            return (pairs[32 * j:32 * j + 32, t % 2, 0:n, s, at], src.rearrange("p g k -> p k g"))

        @block.sync
        def _(sp):
            sp.dma_start(ids_sb[:], ids.rearrange("(t p) f -> p t f", p=P)).then_inc(ids_landed, 16)
            sp.dma_start(ids_int[:], ids_rows).then_inc(id_rows_landed, 16)
            sp.dma_start(pick[:], row_pick).then_inc(id_rows_landed, 16)
            sp.dma_start(row_no[:], row_numbers).then_inc(id_rows_landed, 16)
            for i in range(min(SPLIT_RING, N_ONEHOT)):
                sp.dma_start(table_sb[:, i], onehot_tables[i]).then_inc(table_landed[i], 16)
                if i == 0:
                    sp.dma_start(dense_sb[:], dense.rearrange("(t p) d -> p t d", p=P)).then_inc(dense_landed, 16)
                    sp.dma_start(ident[:], identity).then_inc(dense_landed, 16)
            sp.dma_start(wd2[:], w1_dense).then_inc(wd_landed, 16)
            for i in range(SPLIT_RING, N_ONEHOT):
                sp.wait_ge(lo_ready, i - SPLIT_RING + 1)
                sp.dma_start(table_sb[:, i % SPLIT_RING], onehot_tables[i]).then_inc(table_landed[i % SPLIT_RING], 16)
            sp.dma_start(wp[:], w1_pairs).then_inc(w1_landed, 16)
            sp.dma_start(w2_sb[:], w2).then_inc(mlp_landed, 16)
            sp.dma_start(w3_sb[:], w3).then_inc(mlp_landed, 16)
            sp.dma_start(b1_sb[:], b1).then_inc(mlp_landed, 16)
            sp.dma_start(b2_sb[:], b2).then_inc(mlp_landed, 16)
            sp.wait_ge(y_ready, TILES)
            sp.dma_start(out, y[:]).then_inc(out_written, 16)
            sp.wait_ge(out_written, 16)

        @block.gpsimd
        def _(pool):
            pool.wait_ge(ids_landed, 16)
            for t in range(TILES):
                for g, f in enumerate(GATHERED_TABLES):
                    nc.gpsimd.indirect_dma_start(
                        rows[:, t, g, :], None, tables[f],
                        bass.IndirectOffsetOnAxis(ap=ids_sb[:, t, f:f + 1], axis=0),
                    ).then_inc(rows_landed[t][g // TURN], 16)

        @block.tensor
        def _(pe):
            def take_bank(step):
                n = RING.index(step)
                if n >= 2:
                    pe.wait_ge(drained[drained_by(RING[n - 2])], drains(RING[n - 2]))
                return ring[n % 2]

            for step in STEPS:
                kind = step[0]
                if kind == "dense":
                    bank = take_bank(step)
                    pe.wait_ge(dense_landed, 32)
                    for t in range(TILES):
                        last = nc.tensor.transpose(bank[:, tile(t)], dense_sb[:, t, :], ident[:])
                    last.then_inc(ring_filled, 1)
                elif kind == "ids":
                    i = step[1]
                    bank = take_bank(step)
                    if i == 0:
                        pe.wait_ge(ids_half_ready, 1)
                    nc.tensor.matmul(bank[:], pick[:, i, :], ids_half[:], start=True, stop=True).then_inc(ring_filled, 1)
                elif kind == "onehot":
                    i = step[1]
                    bank = take_bank(step)
                    pe.wait_ge(lo_ready, i + 1)
                    for k in range(ROW_BLOCKS):
                        pe.wait_ge(onehot_ready, i * ROW_BLOCKS + k + 1)
                        for n, part in enumerate((table_hi, table_lo)):
                            last = nc.tensor.matmul(bank[:], part[:, i % SPLIT_RING, k, :], onehot[:, i % 2, k, :],
                                                    start=(k == 0 and n == 0), stop=(k == ROW_BLOCKS - 1 and n == 1))
                    last.then_inc(ring_filled, 1)
                elif kind == "turn":
                    _, t, q = step
                    bank = take_bank(step)
                    if q == 0 and t == 0:
                        pe.wait_ge(dense_landed, 32)
                    pe.wait_ge(rows_landed[t][q], 16 * len(turned(q)))
                    for n, g in enumerate(turned(q)):
                        last = nc.tensor.transpose(bank[:, n * P:(n + 1) * P], rows[:, t, g, :], ident[:])
                    last.then_inc(ring_filled, 1)
                elif kind == "gram":
                    _, t, half = step
                    if half == 0:
                        pe.wait_ge(cleared, 2)
                        for who in ("scalar", "vector"):
                            mine = [s for s in RING if drained_by(s) == who and not (s[0] == "turn" and s[1] > t)]
                            pe.wait_ge(drained[who], drains(mine[-1]))
                    chunk = 2 * t + half
                    if chunk >= 1:
                        pe.wait_ge(pairs_scalar, chunk)
                        pe.wait_ge(pairs_vector, chunk)
                    for g in range(GROUPS):
                        b = t * P + (half * GROUPS + g) * QUADS
                        last = nc.tensor.matmul(
                            gram[:, g, 0:QUADS * COLUMNS],
                            eT[:, b:b + QUADS, :].rearrange("p b f -> p (b f)"),
                            eT[:, b:b + QUADS, 1:FEATURES], start=True, stop=True)
                    last.then_inc(gram_filled, 1)
                elif kind == "layer1":
                    t = step[1]
                    if t == 0:
                        pe.wait_ge(w1_landed, 16)
                        pe.wait_ge(wd_ready, 1)
                        pe.wait_ge(dense_copied, 1)
                    pe.wait_ge(pairs_scalar, 2 * t + 2)
                    pe.wait_ge(pairs_vector, 2 * t + 2)
                    if t >= 1:
                        pe.wait_ge(h1_scalar, t)
                        pe.wait_ge(h1_vector, t)
                    for m in range(H1 // P):
                        nc.tensor.matmul(h1_ps[:, m, :], wd[:, tile(m)], denseT[:, t].rearrange("p s g -> p (s g)"),
                                         start=True, stop=False)
                        for k in range(K_TILES):
                            last = nc.tensor.matmul(h1_ps[:, m, :], wp[:, k, tile(m)],
                                                    pairs[:, t % 2, k].rearrange("p s g -> p (s g)"),
                                                    start=False, stop=(k == K_TILES - 1))
                    last.then_inc(h1_filled, 1)
                elif kind == "layer2":
                    t = step[1]
                    if t == 0:
                        pe.wait_ge(mlp_landed, 64)
                    pe.wait_ge(h1_scalar, t + 1)
                    pe.wait_ge(h1_vector, t + 1)
                    if t >= 1:
                        pe.wait_ge(h2_scalar, t)
                        pe.wait_ge(h2_vector, t)
                        pe.wait_ge(y_ready, t)
                    for m in range(H2 // P):
                        for k in range(H1 // P):
                            last = nc.tensor.matmul(h2_ps[:, tile(m)], w2_sb[:, k, tile(m)], h1[:, k, :],
                                                    start=(k == 0), stop=(k == H1 // P - 1))
                    last.then_inc(h2_filled, 1)
                else:
                    t = step[1]
                    pe.wait_ge(h2_scalar, t + 1)
                    pe.wait_ge(h2_vector, t + 1)
                    for k in range(H2 // P):
                        last = nc.tensor.matmul(y_ps, w3_sb[:, k:k + 1], h2[:, k, :],
                                                start=(k == 0), stop=(k == H2 // P - 1))
                    last.then_inc(y_filled, 1)

        @block.scalar
        def _(act):
            def split_high(i):
                act.wait_ge(table_landed[i % SPLIT_RING], 16 * (i // SPLIT_RING + 1))
                if i >= SPLIT_RING:
                    act.wait_ge(ring_filled, RING.index(("onehot", i - SPLIT_RING)) + 1)
                nc.scalar.activation(table_hi[:, i % SPLIT_RING], table_sb[:, i % SPLIT_RING], ACT.Copy).then_inc(hi_ready, 1)

            for step in STEPS:
                kind = step[0]
                if kind in ("dense", "ids", "onehot", "turn"):
                    if drained_by(step) != "scalar":
                        continue
                    if kind == "ids":
                        split_high(step[1])
                    act.wait_ge(ring_filled, RING.index(step) + 1)
                    if kind == "ids":
                        i = step[1]
                        if i >= 2:
                            act.wait_ge(onehot_ready, (i - 1) * ROW_BLOCKS)
                        nc.scalar.activation(ids_bc[:, i % 2, :], drain_source(step), ACT.Copy).then_inc(drained["scalar"], 1)
                    elif kind == "dense":
                        nc.scalar.activation(
                            denseT[:], drain_source(step).rearrange("p (t g s) -> p t s g", t=TILES, s=QUADS),
                            ACT.Copy).then_inc(dense_copied, 1)
                    if kind != "ids":
                        to, _ = drain_target(step)
                        nc.scalar.activation(to, drain_source(step), ACT.Copy).then_inc(drained["scalar"], 1)
                elif kind == "gram":
                    _, t, half = step
                    act.wait_ge(gram_filled, 2 * t + half + 1)
                    if half == 0 and t >= 2:
                        act.wait_ge(h1_filled, t - 1)
                    for s in (0, 1):
                        for j in range(QUADS):
                            to, of = pairs_parts(t, half, s, j)
                            last = nc.scalar.activation(to, of, ACT.Copy)
                    last.then_inc(pairs_scalar, 1)
                elif kind == "layer1":
                    t = step[1]
                    if t == 0:
                        act.wait_ge(mlp_landed, 64)
                    else:
                        act.wait_ge(h2_filled, t)
                    act.wait_ge(h1_filled, t + 1)
                    for m in range(H1 // P):
                        last = nc.scalar.activation(h1[LOW, m, :], h1_ps[LOW, m, :], ACT.Relu, bias=b1_sb[LOW, m:m + 1])
                    last.then_inc(h1_scalar, 1)
                elif kind == "layer2":
                    t = step[1]
                    act.wait_ge(h2_filled, t + 1)
                    if t >= 1:
                        act.wait_ge(y_filled, t)
                    for m in range(H2 // P):
                        last = nc.scalar.activation(h2[LOW, m, :], h2_ps[LOW, tile(m)], ACT.Relu, bias=b2_sb[LOW, m:m + 1])
                    last.then_inc(h2_scalar, 1)
                else:
                    t = step[1]
                    act.wait_ge(y_filled, t + 1)
                    nc.scalar.activation(y[:, tile(t)].rearrange("p (g s) -> p s g", s=QUADS),
                                         y_ps.rearrange("p (s g) -> p s g", s=QUADS), ACT.Copy).then_inc(y_ready, 1)

        @block.vector
        def _(dve):
            nc.vector.memset(eT[:, :, FEATURES:SLOTS], 0.0).then_inc(cleared, 1)
            nc.vector.memset(pairs[64:128, :, K_TILES - 1], 0.0).then_inc(cleared, 1)
            dve.wait_ge(id_rows_landed, 48)
            nc.vector.tensor_copy(ids_half[:], ids_int[:]).then_inc(ids_half_ready, 1)
            for step in STEPS:
                kind = step[0]
                if kind == "ids":
                    i = step[1]
                    slot = i % SPLIT_RING
                    dve.wait_ge(hi_ready, i + 1)
                    if i >= SPLIT_RING:
                        dve.wait_ge(ring_filled, RING.index(("onehot", i - SPLIT_RING)) + 1)
                    nc.vector.tensor_tensor(table_lo[:, slot], table_sb[:, slot], table_hi[:, slot].bitcast(f32),
                                            ALU.subtract).then_inc(lo_ready, 1)
                    dve.wait_ge(drained["scalar"], drains(step))
                    if i >= 2:
                        dve.wait_ge(ring_filled, RING.index(("onehot", i - 2)) + 1)
                    for k in range(ROW_BLOCKS):
                        nc.vector.tensor_scalar(onehot[:, i % 2, k, :], ids_bc[:, i % 2, :], row_no[:, k:k + 1], None,
                                                ALU.is_equal).then_inc(onehot_ready, 1)
                elif kind == "turn" and drained_by(step) == "vector":
                    dve.wait_ge(ring_filled, RING.index(step) + 1)
                    to, _ = drain_target(step)
                    nc.vector.tensor_copy(to, drain_source(step)).then_inc(drained["vector"], 1)
                elif kind == "gram":
                    _, t, half = step
                    if t == 0 and half == 0:
                        dve.wait_ge(wd_landed, 16)
                        nc.vector.tensor_tensor(wd[:], wd2[:, 0], wd2[:, 1], ALU.add).then_inc(wd_ready, 1)
                    dve.wait_ge(gram_filled, 2 * t + half + 1)
                    if half == 0 and t >= 2:
                        dve.wait_ge(h1_filled, t - 1)
                    for s in (2, 3):
                        for j in range(QUADS):
                            to, of = pairs_parts(t, half, s, j)
                            last = nc.vector.tensor_copy(to, of)
                    last.then_inc(pairs_vector, 1)
                elif kind == "layer1":
                    t = step[1]
                    if t == 0:
                        dve.wait_ge(mlp_landed, 64)
                    else:
                        dve.wait_ge(h2_filled, t)
                    dve.wait_ge(h1_filled, t + 1)
                    for m in range(H1 // P):
                        last = nc.vector.tensor_scalar(h1[HIGH, m, :], h1_ps[HIGH, m, :], b1_sb[HIGH, m:m + 1], 0.0,
                                                       ALU.add, ALU.max)
                    last.then_inc(h1_vector, 1)
                elif kind == "layer2":
                    t = step[1]
                    dve.wait_ge(h2_filled, t + 1)
                    if t >= 1:
                        dve.wait_ge(y_filled, t)
                    for m in range(H2 // P):
                        last = nc.vector.tensor_scalar(h2[HIGH, m, :], h2_ps[HIGH, tile(m)], b2_sb[HIGH, m:m + 1], 0.0,
                                                       ALU.add, ALU.max)
                    last.then_inc(h2_vector, 1)


def layouts(inputs):
    import numpy as np

    def array(name):
        return np.ascontiguousarray(inputs[name])

    w1 = array("W_top1")
    w1_pairs = np.zeros((QUADS, SLOTS, K_TILES, H1), w1.dtype)
    feature = [0] + [1 + f for f in SLOT_TABLE]
    first = {}
    row = D
    for f in range(FEATURES):
        for g in range(f + 1, FEATURES):
            first[f, g] = row
            row += 1
    for c in range(1, FEATURES):
        for r in range(c):
            a, b = sorted((feature[r], feature[c]))
            w1_pairs[(c - 1) % QUADS, r, (c - 1) // QUADS] = w1[first[a, b]]
    onehot_tables = np.zeros((N_ONEHOT, TABLE_ROWS, D), w1.dtype)
    for i, f in enumerate(ONEHOT_TABLES):
        table = array(f"tbl_{f}")
        onehot_tables[i, :len(table)] = table
    ids = array("ids")
    out = {
        "dense": array("r_dense_features"),
        "ids": ids,
        "ids_rows": np.ascontiguousarray(ids.T[list(ONEHOT_TABLES)]),
        "onehot_tables": onehot_tables.reshape(N_ONEHOT, P, ROW_BLOCKS, D),
        "w1_dense": np.ascontiguousarray(np.stack([w1[:D], w1[row:row + D]], axis=1)),
        "w1_pairs": w1_pairs.reshape(P, K_TILES, H1),
        "w2": np.ascontiguousarray(array("W_top2").reshape(H1 // P, P, H2).transpose(1, 0, 2)),
        "w3": np.ascontiguousarray(array("W_top3").reshape(H2 // P, P).T),
        "b1": np.ascontiguousarray(array("b_top1").reshape(H1 // P, P).T),
        "b2": np.ascontiguousarray(array("b_top2").reshape(H2 // P, P).T),
        "identity": np.eye(P, dtype=np.float32),
        "row_numbers": np.arange(TABLE_ROWS, dtype=np.float32).reshape(P, ROW_BLOCKS),
        "row_pick": np.repeat(np.eye(N_ONEHOT, dtype=np.float16)[:, :, None], P, axis=2),
    }
    for f in GATHERED_TABLES:
        out[f"tbl_{f}"] = array(f"tbl_{f}")
    return out


def kernel(**inputs):
    import numpy as np
    import concourse.bacc as bacc
    from concourse.bass_utils import run_bass_kernel_spmd

    nc = bacc.Bacc("TRN2", target_bir_lowering=False, num_devices=1)
    arrays, aps = {}, {}
    for name, a in layouts(inputs).items():
        arrays[f"in_{name}"] = a
        aps[name] = nc.dram_tensor(f"in_{name}", a.shape, mybir.dt.from_np(a.dtype), kind="ExternalInput").ap()
    out = nc.dram_tensor("out", (1, BATCH), mybir.dt.float32, kind="ExternalOutput").ap()
    tables = {f: aps.pop(f"tbl_{f}") for f in GATHERED_TABLES}
    dlrm_tower(nc, tables=tables, out=out, **aps)
    result = run_bass_kernel_spmd(nc, [arrays], core_ids=[0])
    return result.results[0]["out"].reshape(BATCH, 1)
```

```python
import concourse.bass as bass
from concourse import mybir
from contextlib import ExitStack

P = 128
BATCH, D = 512, 128
TABLES = 26
TILES = BATCH // P
FEATURES = TABLES + 1
SLOTS = 32
H1, H2 = 512, 256

ONEHOT_TABLES = (0, 2, 4, 6, 10, 12, 15)
GATHERED_TABLES = tuple(f for f in range(TABLES) if f not in ONEHOT_TABLES)
SLOT_TABLE = ONEHOT_TABLES + GATHERED_TABLES
N_ONEHOT, N_GATHERED = len(ONEHOT_TABLES), len(GATHERED_TABLES)
TABLE_ROWS = 1024
ROW_BLOCKS = TABLE_ROWS // P

TURN = 4
TURNS = -(-N_GATHERED // TURN)
SPAN = FEATURES // 2
PACKED = SPAN + 1
QUADS = 4
SCALAR_QUADS = 2
CHUNKS = 4
GROUPS = P // QUADS // CHUNKS
K_TILES = -(-PACKED // QUADS)
GRAM_ROWS = (QUADS - 1) * SLOTS + FEATURES
A, B = 0, 1
SCALAR_BLOCKS = 1
VECTOR_BLOCKS = ROW_BLOCKS - SCALAR_BLOCKS
STAGE_RING = 3
SPLIT_RING = 2
WIDE = ROW_BLOCKS * D
W_STAGES = -(-K_TILES * H1 // WIDE)
STAGES = N_ONEHOT + W_STAGES + 1
EARLY_SPLITS = 2
FIRST_TURN = 1
SCALAR_STAGES = 2


def packed_in(j):
    return len(range(j, PACKED, QUADS))


def from_b(i, r):
    return i <= r < i + SPAN


def packed_pair(i, r):
    if from_b(i, r):
        return r, i + SPAN
    if i < SPAN and r != i + SPAN:
        return r, i
    return None


def schedule():
    steps = [("ids", 0), ("dense",)]
    splits = [("split_w", n) for n in range(W_STAGES + 1)]
    turns = [("turn", 0, q) for q in range(TURNS)]
    for i in range(N_ONEHOT):
        if i + 1 < N_ONEHOT:
            steps.append(("ids", i + 1))
        steps.append(("onehot", i))
        if i >= N_ONEHOT - EARLY_SPLITS:
            steps.append(splits.pop(0))
        if i >= FIRST_TURN and turns:
            steps.append(turns.pop(0))
    while turns or splits:
        steps += splits[:1] + turns[:1]
        del splits[:1], turns[:1]
    for t in range(TILES):
        turns = [("turn", t + 1, q) for q in range(TURNS)] if t + 1 < TILES else []
        for c in range(CHUNKS):
            steps.append(("gram", t, c))
            if t >= 1 and c == 0:
                steps += [("turn_h1", t - 1, 0), ("turn_h1", t - 1, 1)]
            if turns:
                steps.append(turns.pop(0))
            steps.append(("pack", t, c))
        if t >= 1:
            steps.append(("layer2", t - 1))
        steps += turns
        steps.append(("layer1", t))
    steps += [("turn_h1", TILES - 1, 0), ("turn_h1", TILES - 1, 1), ("layer2", TILES - 1), ("turn_y",)]
    return steps


STEPS = schedule()
RING = [s for s in STEPS if s[0] in ("dense", "onehot", "turn", "turn_h1", "turn_y")]


def drained_by(step):
    if step[0] in ("turn", "turn_h1") and step[2] % 2 == 1:
        return "vector"
    return "scalar"


def drains(step):
    upto = RING[: RING.index(step) + 1]
    return sum(drained_by(s) == drained_by(step) for s in upto)


def dlrm_tower(nc, dense, ids, ids_rows, tables, onehot_tables, w1_dense, w1_pairs, w2, w3, b1, b2,
               identity, row_numbers, row_pick, packed_from_b, out):
    f32, f32r, f16, i32 = (mybir.dt.float32, mybir.dt.float32r, mybir.dt.float16, mybir.dt.int32)
    ALU = mybir.AluOpType
    ACT = mybir.ActivationFunctionType

    ctx = ExitStack()
    with ctx:
        def sb(name, shape, dt):
            return ctx.enter_context(nc.sbuf_tensor(name, shape, dt))

        def psum(name, shape):
            return ctx.enter_context(nc.psum_tensor(name, shape, f32))

        def sem(name):
            return ctx.enter_context(nc.semaphore(name))

        ids_sb = sb("ids_sb", [P, TILES, TABLES], i32)
        ids_int = sb("ids_int", [N_ONEHOT, BATCH], i32)
        ids_half = sb("ids_half", [N_ONEHOT, BATCH], f16)
        pick = sb("pick", [N_ONEHOT, N_ONEHOT, P], f16)
        ident = sb("ident", [P, P], f32)
        row_no = sb("row_no", [P, ROW_BLOCKS], f32)
        rows = sb("rows", [P, 2, N_GATHERED, D], f32)
        staged = sb("staged", [P, STAGE_RING, WIDE], f32)
        table_hi = sb("table_hi", [P, SPLIT_RING, ROW_BLOCKS, D], f32r)
        table_lo = sb("table_lo", [P, SPLIT_RING, ROW_BLOCKS, D], f32r)
        ids_bc = sb("ids_bc", [P, 2, BATCH], f16)
        distance = sb("distance", [P, SCALAR_BLOCKS, BATCH], f16)
        minus_row_no = sb("minus_row_no", [P, ROW_BLOCKS], f32)
        onehot = sb("onehot", [P, 2, ROW_BLOCKS, BATCH], f32r)
        eT = sb("eT", [P, BATCH, SLOTS], f32)
        denseT = sb("denseT", [P, TILES, QUADS, P // QUADS], f32)
        pairs = sb("pairs", [P, 2, K_TILES, QUADS, P // QUADS], f32)
        b_mask = sb("b_mask", [P, K_TILES, P // CHUNKS], i32)
        denseT_hi = sb("denseT_hi", [P, TILES, P], f32r)
        denseT_lo = sb("denseT_lo", [P, TILES, P], f32r)
        pairs_hi = sb("pairs_hi", [P, K_TILES, QUADS, P // QUADS], f32r)
        pairs_lo = sb("pairs_lo", [P, K_TILES, QUADS, P // QUADS], f32r)
        wd = sb("wd", [P, H1], f32)
        w1_hi = sb("w1_hi", [P, K_TILES + 1, H1], f32r)
        w1_lo = sb("w1_lo", [P, K_TILES + 1, H1], f32r)
        w2_sb = sb("w2_sb", [P, H1 // P, H2], f32)
        w3_bc = sb("w3_bc", [P, H2], f32)
        b2_bc = sb("b2_bc", [P, H2], f32)
        b1_sb = sb("b1_sb", [P, H1 // P], f32)
        h1_rows = sb("h1_rows", [P, H1], f32)
        dense_sb = h1_rows[:].rearrange("p (t d) -> p t d", t=TILES)
        h1 = sb("h1", [P, H1 // P, P], f32)
        h2 = sb("h2", [P, 2, H2], f32)
        y_cols = sb("y_cols", [P, TILES], f32)
        y = sb("y", [TILES, P], f32)

        ring = [psum(f"ring{n}", [P, 512]) for n in range(2)]
        gram = psum("gram", [P, 2, GROUPS, P])
        banks = psum("banks", [P, 2, 512])
        h1_ps = [banks[:, 0, 0:H1 // 2], banks[:, 1, 0:H1 // 2]]
        h2_ps = banks[:, 1, H1 // 2:H1 // 2 + H2]

        ids_landed = sem("ids_landed")
        id_rows_landed = sem("id_rows_landed")
        row_no_landed = sem("row_no_landed")
        pick_landed = sem("pick_landed")
        dense_landed = sem("dense_landed")
        stage_landed = [sem(f"stage_landed{n}") for n in range(STAGE_RING)]
        mask_landed = sem("mask_landed")
        mlp_landed = sem("mlp_landed")
        rows_landed = [[sem(f"rows_landed{t}_{q}") for q in range(TURNS)] for t in range(TILES)]
        out_written = sem("out_written")

        cleared = sem("cleared")
        ids_half_ready = sem("ids_half_ready")
        hi_ready = sem("hi_ready")
        lo_ready = sem("lo_ready")
        onehot_ready = sem("onehot_ready")
        distance_ready = sem("distance_ready")
        scalar_onehot_ready = sem("scalar_onehot_ready")
        wd_ready = sem("wd_ready")
        ring_filled = sem("ring_filled")
        ids_filled = sem("ids_filled")
        ids_copied = sem("ids_copied")
        drained = {"scalar": sem("drained_scalar"), "vector": sem("drained_vector")}
        dense_copied = sem("dense_copied")
        dense_lo_ready = sem("dense_lo_ready")
        gram_filled = sem("gram_filled")
        pairs_scalar = sem("pairs_scalar")
        pairs_vector = sem("pairs_vector")
        pairs_merged = sem("pairs_merged")
        pairs_hi_ready = sem("pairs_hi_ready")
        pairs_lo_ready = sem("pairs_lo_ready")
        h1_filled = sem("h1_filled")
        h1_copied = sem("h1_copied")
        h2_filled = sem("h2_filled")
        h2_read = sem("h2_read")
        y_ready = sem("y_ready")

        block = ctx.enter_context(nc.Block())

        def tile(t):
            return slice(t * P, (t + 1) * P)

        def turned(q):
            return range(q * TURN, min((q + 1) * TURN, N_GATHERED))

        def drain_target(step):
            if step[0] == "dense":
                return eT[:, :, 0]
            if step[0] == "onehot":
                return eT[:, :, 1 + step[1]]
            _, t, q = step
            slot = 1 + N_ONEHOT + q * TURN
            n = len(turned(q))
            return eT[:, tile(t), slot:slot + n].rearrange("p b f -> p f b")

        def drain_source(step):
            bank = ring[RING.index(step) % 2]
            if step[0] == "turn":
                n = len(turned(step[2]))
                return bank[:, 0:n * P].rearrange("p (f b) -> p f b", f=n)
            return bank[:, 0:BATCH]

        def groups(c):
            return slice(c * GROUPS, (c + 1) * GROUPS)

        def pairs_parts(c, s, j):
            n = packed_in(j)
            block = gram[SLOTS * s:SLOTS * s + FEATURES, c % 2, :, s * FEATURES + j:s * FEATURES + j + SPAN + QUADS * (n - 1) + 1]
            src = bass.AP(tensor=block.tensor, offset=block.offset,
                          ap=[block.ap[0], [SPAN, 2], [QUADS, n], [P, GROUPS]])
            return pairs[SLOTS * j:SLOTS * j + FEATURES, :, 0:n, s, groups(c)], src

        def chunk_of(part, c):
            return part[:, :, :, groups(c)]

        def stage_parts(n):
            slot = n % SPLIT_RING
            stage = n % STAGE_RING
            if n < N_ONEHOT:
                return (staged[:, stage].rearrange("p (k d) -> p k d", d=D), table_hi[:, slot], table_lo[:, slot])
            if n == STAGES - 1:
                return wd[:], w1_hi[:, K_TILES], w1_lo[:, K_TILES]
            k = slice((n - N_ONEHOT) * (WIDE // H1), min((n - N_ONEHOT + 1) * (WIDE // H1), K_TILES))
            size = k.stop - k.start
            return (staged[:, stage, 0:size * H1].rearrange("p (k m) -> p k m", m=H1), w1_hi[:, k], w1_lo[:, k])

        def stage_source(n):
            if n < N_ONEHOT:
                return onehot_tables[n]
            if n == STAGES - 1:
                return w1_dense
            at = (n - N_ONEHOT) * WIDE
            return w1_pairs[:, at:min(at + WIDE, K_TILES * H1)]

        def load_stage(queue, n):
            source = stage_source(n)
            queue.dma_start(staged[:, n % STAGE_RING, 0:source.shape[1]], source).then_inc(stage_landed[n % STAGE_RING], 16)

        @block.sync
        def _(sp):
            sp.dma_start(ids_int[:], ids_rows).then_inc(id_rows_landed, 16)
            sp.dma_start(ids_sb[:], ids.rearrange("(t p) f -> p t f", p=P)).then_inc(ids_landed, 16)
            sp.dma_start(pick[:], row_pick).then_inc(pick_landed, 16)
            sp.dma_start(row_no[:], row_numbers).then_inc(row_no_landed, 16)
            sp.dma_start(ident[:], identity).then_inc(dense_landed, 16)
            for n in range(SCALAR_STAGES, STAGES):
                if n >= STAGE_RING:
                    sp.wait_ge(lo_ready, n - STAGE_RING + 1)
                load_stage(sp, n)
            sp.dma_start(b_mask[:], packed_from_b).then_inc(mask_landed, 16)
            sp.dma_start(w2_sb[:], w2).then_inc(mlp_landed, 16)
            sp.dma_start(w3_bc[:], w3.to_broadcast((P, H2))).then_inc(mlp_landed, 16)
            sp.dma_start(b1_sb[:], b1).then_inc(mlp_landed, 16)
            sp.dma_start(b2_bc[:], b2.to_broadcast((P, H2))).then_inc(mlp_landed, 16)
            sp.wait_ge(drained["scalar"], drains(("turn_y",)))
            sp.dma_start(out, y[:]).then_inc(out_written, 16)
            sp.wait_ge(out_written, 16)

        @block.gpsimd
        def _(pool):
            nc.gpsimd.memset(eT[:, :, FEATURES:SLOTS], 0.0).then_inc(cleared, 1)
            pool.wait_ge(ids_landed, 16)
            for t in range(TILES):
                for g, f in enumerate(GATHERED_TABLES):
                    if t >= 2 and g % TURN == 0:
                        pool.wait_ge(ring_filled, RING.index(("turn", t - 2, g // TURN)) + 1)
                    nc.gpsimd.indirect_dma_start(
                        rows[:, t % 2, g, :], None, tables[f],
                        bass.IndirectOffsetOnAxis(ap=ids_sb[:, t, f:f + 1], axis=0),
                    ).then_inc(rows_landed[t][g // TURN], 16)

        @block.tensor
        def _(pe):
            def take_bank(step):
                n = RING.index(step)
                if n >= 2:
                    pe.wait_ge(drained[drained_by(RING[n - 2])], drains(RING[n - 2]))
                return ring[n % 2]

            for step in STEPS:
                kind = step[0]
                if kind == "dense":
                    bank = take_bank(step)
                    pe.wait_ge(dense_landed, 32)
                    for t in range(TILES):
                        last = nc.tensor.transpose(bank[:, tile(t)], dense_sb[:, t, :], ident[:])
                    last.then_inc(ring_filled, 1)
                elif kind == "ids":
                    i = step[1]
                    if i == 0:
                        pe.wait_ge(pick_landed, 16)
                        pe.wait_ge(ids_half_ready, 1)
                    else:
                        pe.wait_ge(ids_copied, i)
                    nc.tensor.matmul(banks[:, 0, :], pick[:, i, :], ids_half[:], start=True, stop=True).then_inc(ids_filled, 1)
                elif kind == "onehot":
                    i = step[1]
                    bank = take_bank(step)
                    for n, (part, ready) in enumerate(((table_hi, hi_ready), (table_lo, lo_ready))):
                        pe.wait_ge(ready, i + 1)
                        for k in range(ROW_BLOCKS):
                            if n == 0:
                                if k < VECTOR_BLOCKS:
                                    pe.wait_ge(onehot_ready, i * VECTOR_BLOCKS + k + 1)
                                else:
                                    pe.wait_ge(scalar_onehot_ready, i * SCALAR_BLOCKS + k - VECTOR_BLOCKS + 1)
                            last = nc.tensor.matmul(bank[:], part[:, i % SPLIT_RING, k, :], onehot[:, i % 2, k, :],
                                                    start=(k == 0 and n == 0), stop=(k == ROW_BLOCKS - 1 and n == 1))
                    last.then_inc(ring_filled, 1)
                elif kind == "turn":
                    _, t, q = step
                    bank = take_bank(step)
                    if q == 0 and t == 0:
                        pe.wait_ge(dense_landed, 32)
                    pe.wait_ge(rows_landed[t][q], 16 * len(turned(q)))
                    for n, g in enumerate(turned(q)):
                        last = nc.tensor.transpose(bank[:, n * P:(n + 1) * P], rows[:, t % 2, g, :], ident[:])
                    last.then_inc(ring_filled, 1)
                elif kind == "gram":
                    _, t, c = step
                    if c == 0:
                        pe.wait_ge(cleared, 2)
                        for who in ("scalar", "vector"):
                            slots = [s for s in RING if s[0] in ("dense", "onehot") or s[:2] == ("turn", t)]
                            pe.wait_ge(drained[who], max(drains(s) for s in slots if drained_by(s) == who))
                    chunk = CHUNKS * t + c
                    if chunk >= 2:
                        pe.wait_ge(pairs_scalar, chunk - 1)
                        pe.wait_ge(pairs_vector, chunk - 1)
                    for g in range(GROUPS):
                        b = t * P + (c * GROUPS + g) * QUADS
                        last = nc.tensor.matmul(
                            gram[0:GRAM_ROWS, c % 2, g, 0:QUADS * FEATURES],
                            eT[:, b:b + QUADS, :].rearrange("p b f -> p (b f)")[:, 0:GRAM_ROWS],
                            eT[:, b:b + QUADS, 0:FEATURES], start=True, stop=True)
                    last.then_inc(gram_filled, 1)
                elif kind == "layer1":
                    t = step[1]
                    if t == 0:
                        pe.wait_ge(lo_ready, STAGES)
                        pe.wait_ge(dense_lo_ready, 1)
                        pe.wait_ge(ids_copied, N_ONEHOT)
                    else:
                        pe.wait_ge(h1_copied, 2 * t)
                        pe.wait_ge(h2_read, t)
                    k_tiles = [(denseT_hi[:, t], denseT_lo[:, t])]
                    k_tiles += [(pairs_hi[:, k].rearrange("p s g -> p (s g)"), pairs_lo[:, k].rearrange("p s g -> p (s g)"))
                                for k in range(K_TILES)]
                    for half in range(2):
                        m = slice(half * H1 // 2, (half + 1) * H1 // 2)
                        for n, (high, low) in enumerate(k_tiles):
                            if half == 0 and n == 1:
                                pe.wait_ge(pairs_lo_ready, CHUNKS * (t + 1))
                            k = (n - 1) % (K_TILES + 1)
                            nc.tensor.matmul(h1_ps[half], high, w1_hi[:, k, m], start=(n == 0), stop=False)
                            nc.tensor.matmul(h1_ps[half], high, w1_lo[:, k, m], start=False, stop=False)
                            last = nc.tensor.matmul(h1_ps[half], low, w1_hi[:, k, m], start=False, stop=(n == K_TILES))
                        last.then_inc(h1_filled, 1)
                elif kind == "turn_h1":
                    _, t, half = step
                    bank = take_bank(step)
                    pe.wait_ge(h1_copied, 2 * t + half + 1)
                    for m in range(2):
                        last = nc.tensor.transpose(bank[:, tile(m)], h1_rows[:, tile(2 * half + m)], ident[:])
                    last.then_inc(ring_filled, 1)
                elif kind == "layer2":
                    t = step[1]
                    if t == 0:
                        pe.wait_ge(mlp_landed, 64)
                    for k in range(H1 // P):
                        if k % 2 == 0:
                            h1_turn = ("turn_h1", t, k // 2)
                            pe.wait_ge(drained[drained_by(h1_turn)], drains(h1_turn))
                        last = nc.tensor.matmul(h2_ps, h1[:, k, :], w2_sb[:, k, :], start=(k == 0), stop=(k == H1 // P - 1))
                    last.then_inc(h2_filled, 1)
                elif kind == "turn_y":
                    bank = take_bank(step)
                    pe.wait_ge(y_ready, TILES)
                    nc.tensor.transpose(bank[0:TILES, 0:P], y_cols[:], ident[:]).then_inc(ring_filled, 1)

        @block.scalar
        def _(act):
            def split_high(n):
                if n == STAGES - 1:
                    act.wait_ge(wd_ready, 1)
                else:
                    act.wait_ge(stage_landed[n % STAGE_RING], 16 * (n // STAGE_RING + 1))
                if SPLIT_RING <= n < N_ONEHOT:
                    act.wait_ge(ring_filled, RING.index(("onehot", n - SPLIT_RING)) + 1)
                whole, high, _ = stage_parts(n)
                nc.scalar.activation(high, whole, ACT.Copy).then_inc(hi_ready, 1)

            for n in range(SCALAR_STAGES):
                load_stage(act, n)
                if n == 0:
                    act.dma_start(dense_sb, dense.rearrange("(t p) d -> p t d", p=P)).then_inc(dense_landed, 16)
            for step in STEPS:
                kind = step[0]
                if kind == "ids":
                    i = step[1]
                    act.wait_ge(ids_filled, i + 1)
                    if i >= 2:
                        act.wait_ge(onehot_ready, (i - 1) * VECTOR_BLOCKS)
                        act.wait_ge(distance_ready, (i - 1) * SCALAR_BLOCKS)
                    nc.scalar.activation(ids_bc[:, i % 2, :], banks[:, 0, :], ACT.Copy).then_inc(ids_copied, 1)
                    split_high(i)
                    act.wait_ge(ids_copied, i + 1)
                    if i == 0:
                        act.wait_ge(ids_half_ready, 2)
                    for n in range(SCALAR_BLOCKS):
                        k = VECTOR_BLOCKS + n
                        if i >= 1:
                            act.wait_ge(scalar_onehot_ready, (i - 1) * SCALAR_BLOCKS + n + 1)
                        nc.scalar.activation(distance[:, n, :], ids_bc[:, i % 2, :], ACT.Abs,
                                             bias=minus_row_no[:, k:k + 1]).then_inc(distance_ready, 1)
                    if i >= 2:
                        act.wait_ge(ring_filled, RING.index(("onehot", i - 2)) + 1)
                    for n in range(SCALAR_BLOCKS):
                        act.wait_ge(distance_ready, i * SCALAR_BLOCKS + n + 1)
                        nc.scalar.activation(onehot[:, i % 2, VECTOR_BLOCKS + n, :], distance[:, n, :], ACT.Relu,
                                             bias=1.0, scale=-1.0).then_inc(scalar_onehot_ready, 1)
                elif kind == "split_w":
                    split_high(N_ONEHOT + step[1])
                elif kind == "dense":
                    act.wait_ge(ring_filled, RING.index(step) + 1)
                    nc.scalar.activation(
                        denseT[:], drain_source(step).rearrange("p (t g s) -> p t s g", t=TILES, s=QUADS),
                        ACT.Copy).then_inc(dense_copied, 1)
                    nc.scalar.activation(drain_target(step), drain_source(step), ACT.Copy).then_inc(drained["scalar"], 1)
                    act.wait_ge(dense_copied, 1)
                    nc.scalar.activation(denseT_hi[:], denseT[:].rearrange("p t s g -> p t (s g)"),
                                         ACT.Copy).then_inc(dense_copied, 1)
                elif kind in ("onehot", "turn") and drained_by(step) == "scalar":
                    act.wait_ge(ring_filled, RING.index(step) + 1)
                    nc.scalar.activation(drain_target(step), drain_source(step), ACT.Copy).then_inc(drained["scalar"], 1)
                elif kind == "gram":
                    _, t, c = step
                    chunk = CHUNKS * t + c
                    act.wait_ge(gram_filled, chunk + 1)
                    if t >= 1 and c == 0:
                        act.wait_ge(pairs_lo_ready, CHUNKS * t)
                    if chunk == 0:
                        act.wait_ge(cleared, 2)
                    for s in range(SCALAR_QUADS):
                        for j in range(QUADS):
                            to, of = pairs_parts(c, s, j)
                            last = nc.scalar.activation(to, of, ACT.Copy)
                    last.then_inc(pairs_scalar, 1)
                elif kind == "pack":
                    _, t, c = step
                    chunk = CHUNKS * t + c
                    act.wait_ge(pairs_merged, chunk + 1)
                    if t >= 1 and c == 0:
                        act.wait_ge(h1_filled, 2 * t)
                    nc.scalar.activation(chunk_of(pairs_hi, c), chunk_of(pairs[:, A], c), ACT.Copy).then_inc(pairs_hi_ready, 1)
                elif kind == "turn_h1" and drained_by(step) == "scalar":
                    _, t, half = step
                    if t == 0:
                        act.wait_ge(mlp_landed, 64)
                    else:
                        act.wait_ge(h2_filled, t)
                    act.wait_ge(ring_filled, RING.index(step) + 1)
                    for m in (2 * half, 2 * half + 1):
                        last = nc.scalar.activation(h1[:, m, :], ring[RING.index(step) % 2][:, tile(m % 2)], ACT.Relu,
                                                    bias=b1_sb[:, m:m + 1])
                    last.then_inc(drained["scalar"], 1)
                elif kind == "turn_y":
                    act.wait_ge(ring_filled, RING.index(step) + 1)
                    nc.scalar.activation(y[:].rearrange("t (g s) -> t s g", s=QUADS),
                                         ring[RING.index(step) % 2][0:TILES, 0:P].rearrange("t (s g) -> t s g", s=QUADS),
                                         ACT.Copy).then_inc(drained["scalar"], 1)

        @block.vector
        def _(dve):
            nc.vector.memset(pairs[:], 0.0).then_inc(cleared, 1)
            dve.wait_ge(id_rows_landed, 16)
            nc.vector.tensor_copy(ids_half[:], ids_int[:]).then_inc(ids_half_ready, 1)
            dve.wait_ge(row_no_landed, 16)
            nc.vector.tensor_scalar(minus_row_no[:], row_no[:], -1.0, None, ALU.mult).then_inc(ids_half_ready, 1)
            def split_low(n):
                if n == STAGES - 1:
                    dve.wait_ge(stage_landed[n % STAGE_RING], 16 * (n // STAGE_RING + 1))
                    nc.vector.tensor_tensor(wd[:], staged[:, n % STAGE_RING, 0:H1], staged[:, n % STAGE_RING, H1:2 * H1],
                                            ALU.add).then_inc(wd_ready, 1)
                dve.wait_ge(hi_ready, n + 1)
                if SPLIT_RING <= n < N_ONEHOT:
                    dve.wait_ge(ring_filled, RING.index(("onehot", n - SPLIT_RING)) + 1)
                whole, high, low = stage_parts(n)
                nc.vector.tensor_tensor(low, whole, high.bitcast(f32), ALU.subtract).then_inc(lo_ready, 1)

            def pack_low(t, c):
                dve.wait_ge(pairs_hi_ready, CHUNKS * t + c + 1)
                if t >= 1 and c == 0:
                    dve.wait_ge(h1_filled, 2 * t)
                nc.vector.tensor_tensor(chunk_of(pairs_lo, c), chunk_of(pairs[:, A], c), chunk_of(pairs_hi, c).bitcast(f32),
                                        ALU.subtract).then_inc(pairs_lo_ready, 1)

            for step in STEPS:
                kind = step[0]
                if kind == "ids":
                    i = step[1]
                    dve.wait_ge(ids_copied, i + 1)
                    if i >= 2:
                        dve.wait_ge(ring_filled, RING.index(("onehot", i - 2)) + 1)
                    for k in range(VECTOR_BLOCKS):
                        nc.vector.tensor_scalar(onehot[:, i % 2, k, :], ids_bc[:, i % 2, :], row_no[:, k:k + 1], None,
                                                ALU.is_equal).then_inc(onehot_ready, 1)
                    split_low(i)
                elif kind == "split_w":
                    split_low(N_ONEHOT + step[1])
                    if step[1] == 0:
                        dve.wait_ge(dense_copied, 2)
                        nc.vector.tensor_tensor(denseT_lo[:], denseT[:].rearrange("p t s g -> p t (s g)"),
                                                denseT_hi[:].bitcast(f32), ALU.subtract).then_inc(dense_lo_ready, 1)
                elif kind == "turn" and drained_by(step) == "vector":
                    dve.wait_ge(ring_filled, RING.index(step) + 1)
                    nc.vector.tensor_copy(drain_target(step), drain_source(step)).then_inc(drained["vector"], 1)
                elif kind == "gram":
                    _, t, c = step
                    chunk = CHUNKS * t + c
                    dve.wait_ge(gram_filled, chunk + 1)
                    if t >= 1 and c == 0:
                        dve.wait_ge(pairs_lo_ready, CHUNKS * t)
                    if chunk == 0:
                        dve.wait_ge(cleared, 2)
                    for s in range(SCALAR_QUADS, QUADS):
                        for j in range(QUADS):
                            to, of = pairs_parts(c, s, j)
                            last = nc.vector.tensor_copy(to, of)
                    last.then_inc(pairs_vector, 1)
                elif kind == "pack":
                    _, t, c = step
                    chunk = CHUNKS * t + c
                    if chunk == 0:
                        dve.wait_ge(mask_landed, 16)
                    dve.wait_ge(pairs_scalar, chunk + 1)
                    dve.wait_ge(pairs_vector, chunk + 1)
                    nc.vector.copy_predicated(chunk_of(pairs[:, A], c), b_mask[:].rearrange("p k (s g) -> p k s g", s=QUADS),
                                              chunk_of(pairs[:, B], c)).then_inc(pairs_merged, 1)
                    if c >= 1:
                        pack_low(t, c - 1)
                    if c == CHUNKS - 1:
                        pack_low(t, c)
                elif kind == "layer1":
                    t = step[1]
                    for half in range(2):
                        dve.wait_ge(h1_filled, 2 * t + half + 1)
                        if t >= 1:
                            dve.wait_ge(ring_filled, RING.index(("turn_h1", t - 1, half)) + 1)
                        nc.vector.tensor_copy(h1_rows[:, half * H1 // 2:(half + 1) * H1 // 2], h1_ps[half]).then_inc(h1_copied, 1)
                elif kind == "turn_h1" and drained_by(step) == "vector":
                    _, t, half = step
                    if t == 0:
                        dve.wait_ge(mlp_landed, 64)
                    else:
                        dve.wait_ge(h2_filled, t)
                    dve.wait_ge(ring_filled, RING.index(step) + 1)
                    for m in (2 * half, 2 * half + 1):
                        last = nc.vector.tensor_scalar(h1[:, m, :], ring[RING.index(step) % 2][:, tile(m % 2)],
                                                       b1_sb[:, m:m + 1], 0.0, ALU.add, ALU.max)
                    last.then_inc(drained["vector"], 1)
                elif kind == "layer2":
                    t = step[1]
                    dve.wait_ge(h2_filled, t + 1)
                    if t >= 1:
                        dve.wait_ge(y_ready, t)
                    nc.vector.tensor_tensor(h2[:, 0, :], h2_ps, b2_bc[:], ALU.add).then_inc(h2_read, 1)
                    dve.wait_ge(h2_read, t + 1)
                    nc.vector.scalar_tensor_tensor(h2[:, 1, :], h2[:, 0, :], 0.0, w3_bc[:], ALU.max, ALU.mult,
                                                   accum_out=y_cols[:, t:t + 1]).then_inc(y_ready, 1)


def layouts(inputs):
    import numpy as np

    def array(name):
        return np.ascontiguousarray(inputs[name])

    w1 = array("W_top1")
    w1_pairs = np.zeros((QUADS, SLOTS, K_TILES, H1), w1.dtype)
    feature = [0] + [1 + f for f in SLOT_TABLE]
    first = {}
    row = D
    for f in range(FEATURES):
        for g in range(f + 1, FEATURES):
            first[f, g] = row
            row += 1
    mask = np.zeros((QUADS, SLOTS, K_TILES), np.int32)
    for i in range(PACKED):
        for r in range(FEATURES):
            at = i % QUADS, r, i // QUADS
            mask[at] = from_b(i, r)
            if packed_pair(i, r):
                w1_pairs[at] = w1[first[tuple(sorted(feature[slot] for slot in packed_pair(i, r)))]]
    onehot_tables = np.zeros((N_ONEHOT, TABLE_ROWS, D), w1.dtype)
    for i, f in enumerate(ONEHOT_TABLES):
        table = array(f"tbl_{f}")
        onehot_tables[i, :len(table)] = table
    ids = array("ids")
    out = {
        "dense": array("r_dense_features"),
        "ids": ids,
        "ids_rows": np.ascontiguousarray(ids.T[list(ONEHOT_TABLES)]),
        "onehot_tables": onehot_tables.reshape(N_ONEHOT, P, WIDE),
        "w1_dense": np.concatenate([w1[:D], w1[row:row + D]], axis=1),
        "w1_pairs": w1_pairs.reshape(P, K_TILES * H1),
        "w2": np.ascontiguousarray(array("W_top2").reshape(H1 // P, P, H2).transpose(1, 0, 2)),
        "w3": array("W_top3").reshape(1, H2),
        "b1": np.ascontiguousarray(array("b_top1").reshape(H1 // P, P).T),
        "b2": array("b_top2").reshape(1, H2),
        "identity": np.eye(P, dtype=np.float32),
        "row_numbers": np.arange(TABLE_ROWS, dtype=np.float32).reshape(P, ROW_BLOCKS),
        "packed_from_b": np.repeat(mask.reshape(P, K_TILES, 1), P // CHUNKS, axis=2),
        "row_pick": np.repeat(np.eye(N_ONEHOT, dtype=np.float16)[:, :, None], P, axis=2),
    }
    for f in GATHERED_TABLES:
        out[f"tbl_{f}"] = array(f"tbl_{f}")
    return out


def kernel(**inputs):
    import numpy as np
    import concourse.bacc as bacc
    from concourse.bass_utils import run_bass_kernel_spmd

    nc = bacc.Bacc("TRN2", target_bir_lowering=False, num_devices=1)
    arrays, aps = {}, {}
    for name, a in layouts(inputs).items():
        arrays[f"in_{name}"] = a
        aps[name] = nc.dram_tensor(f"in_{name}", a.shape, mybir.dt.from_np(a.dtype), kind="ExternalInput").ap()
    out = nc.dram_tensor("out", (TILES, P), mybir.dt.float32, kind="ExternalOutput").ap()
    tables = {f: aps.pop(f"tbl_{f}") for f in GATHERED_TABLES}
    dlrm_tower(nc, tables=tables, out=out, **aps)
    result = run_bass_kernel_spmd(nc, [arrays], core_ids=[0])
    return result.results[0]["out"].reshape(BATCH, 1)
```

```python
import concourse.bass as bass
from concourse import mybir
from contextlib import ExitStack

P = 128
BATCH, D = 512, 128
TABLES = 26
TILES = BATCH // P
FEATURES = TABLES + 1
SLOTS = 32
H1, H2 = 512, 256

ONEHOT_TABLES = (0, 2, 4, 6, 10, 12, 15, 16)
GATHERED_TABLES = tuple(f for f in range(TABLES) if f not in ONEHOT_TABLES)
SLOT_TABLE = ONEHOT_TABLES + GATHERED_TABLES
N_ONEHOT, N_GATHERED = len(ONEHOT_TABLES), len(GATHERED_TABLES)
TABLE_ROWS = 1024
ROW_BLOCKS = TABLE_ROWS // P

TURN = 4
TURNS = -(-N_GATHERED // TURN)
SPAN = FEATURES // 2
PACKED = SPAN + 1
QUADS = 4
SCALAR_QUADS = 2
CHUNKS = 4
GROUPS = P // QUADS // CHUNKS
K_TILES = -(-PACKED // QUADS)
GRAM_ROWS = (QUADS - 1) * SLOTS + FEATURES
A, B = 0, 1
SCALAR_BLOCKS = 1
VECTOR_BLOCKS = ROW_BLOCKS - SCALAR_BLOCKS
STAGE_RING = 3
SPLIT_RING = 2
WIDE = ROW_BLOCKS * D
W_STAGES = -(-K_TILES * H1 // WIDE)
STAGES = N_ONEHOT + W_STAGES + 1
WARM_UPS = 12

LOOKUP_STEPS = "OODOOTTOOTTTOSOST"
TILE_STEPS = (("T", "ST", "", "", "TTLLLL"),
              ("TH", "HT", "T", "T", "HHTLLLL"),
              ("HT", "H", "T", "", "HTHLTLLTHL"),
              ("H", "", "", "", "HHLLLHLHHHH"))


def packed_in(j):
    return len(range(j, PACKED, QUADS))


def from_b(i, r):
    return i <= r < i + SPAN


def packed_pair(i, r):
    if from_b(i, r):
        return r, i + SPAN
    if i < SPAN and r != i + SPAN:
        return r, i
    return None


LAYER2 = (("turn_h1", 0, 2), ("turn_h1", 2, 2), ("layer2", 0), ("layer2", 2))
LAST_LAYER2 = (("turn_h1", 0, 2), ("layer2", 0), ("turn_h1", 2, 1), ("turn_h1", 3, 1), ("layer2", 2))


def h1_turn(t, m):
    return next(s for s in RING if s[:2] == ("turn_h1", t) and s[2] <= m < s[2] + s[3])


def schedule():
    later = {
        "O": [("onehot", i) for i in range(N_ONEHOT)],
        "D": [("dense",)],
        "S": [("split_w", n) for n in range(W_STAGES + 1)],
        "T": [("turn", t, q) for t in range(TILES) for q in range(TURNS)],
        "L": [("layer1", t, half, part) for t in range(TILES) for half in range(2) for part in ("high", "low")],
        "H": [(kind, t, *m) for t in range(TILES) for kind, *m in (LAST_LAYER2 if t == TILES - 1 else LAYER2)],
    }
    steps = [("ids", 0)]
    for letter in LOOKUP_STEPS:
        step = later[letter].pop(0)
        if letter == "O" and later["O"]:
            steps.append(("ids", step[1] + 1))
        steps.append(step)
    for t in range(TILES):
        for c in range(CHUNKS):
            steps.append(("gram", t, c))
            steps += [later[letter].pop(0) for letter in TILE_STEPS[t][c]]
            steps.append(("pack", t, c))
        steps += [later[letter].pop(0) for letter in TILE_STEPS[t][CHUNKS]]
    assert not any(later.values())
    return steps


STEPS = schedule()
RING = [s for s in STEPS if s[0] in ("dense", "onehot", "turn", "turn_h1")]


def drained_by(step):
    if step[0] == "turn":
        return ("scalar", "vector")[step[2] % 2]
    if step[0] == "turn_h1":
        return "vector" if step[2] + step[3] == H1 // P else "scalar"
    return "scalar"


def drains(step):
    upto = RING[: RING.index(step) + 1]
    return sum(drained_by(s) == drained_by(step) for s in upto)


def dlrm_tower(nc, dense, ids, ids_rows, tables, onehot_tables, w1_dense, w1_pairs, w2, w3, b1, b2,
               identity, row_numbers, packed_from_b, out):
    f32, f32r, f16, i32 = (mybir.dt.float32, mybir.dt.float32r, mybir.dt.float16, mybir.dt.int32)
    ALU = mybir.AluOpType
    ACT = mybir.ActivationFunctionType

    ctx = ExitStack()
    with ctx:
        def sb(name, shape, dt):
            return ctx.enter_context(nc.sbuf_tensor(name, shape, dt))

        def psum(name, shape):
            return ctx.enter_context(nc.psum_tensor(name, shape, f32))

        def sem(name):
            return ctx.enter_context(nc.semaphore(name))

        ids_sb = sb("ids_sb", [P, TILES, TABLES], i32)
        ids_wide = sb("ids_wide", [P, 2, BATCH], i32)
        ident = sb("ident", [P, P], f32)
        zeros = sb("zeros", [P, 512], f16)
        row_no = sb("row_no", [P, ROW_BLOCKS], f32)
        rows = sb("rows", [P, 2, N_GATHERED, D], f32)
        staged = sb("staged", [P, STAGE_RING, WIDE], f32)
        table_hi = sb("table_hi", [P, SPLIT_RING, ROW_BLOCKS, D], f32r)
        table_lo = sb("table_lo", [P, SPLIT_RING, ROW_BLOCKS, D], f32r)
        ids_bc = sb("ids_bc", [P, 2, BATCH], f16)
        distance = sb("distance", [P, SCALAR_BLOCKS, BATCH], f16)
        minus_row_no = sb("minus_row_no", [P, ROW_BLOCKS], f32)
        onehot = sb("onehot", [P, 2, ROW_BLOCKS, BATCH], f32r)
        eT = sb("eT", [P, BATCH, SLOTS], f32)
        denseT = sb("denseT", [P, TILES, QUADS, P // QUADS], f32)
        pairs = sb("pairs", [P, 2, K_TILES, QUADS, P // QUADS], f32)
        b_mask = sb("b_mask", [P, K_TILES, P // CHUNKS], i32)
        denseT_hi = sb("denseT_hi", [P, TILES, P], f32r)
        denseT_lo = sb("denseT_lo", [P, TILES, P], f32r)
        pairs_hi = sb("pairs_hi", [P, K_TILES, QUADS, P // QUADS], f32r)
        pairs_lo = sb("pairs_lo", [P, K_TILES, QUADS, P // QUADS], f32r)
        wd = sb("wd", [P, H1], f32)
        w1_hi = sb("w1_hi", [P, K_TILES + 1, H1], f32r)
        w1_lo = sb("w1_lo", [P, K_TILES + 1, H1], f32r)
        w2_sb = sb("w2_sb", [P, H1 // P, H2], f32)
        w3_bc = sb("w3_bc", [P, H2], f32)
        b2_bc = sb("b2_bc", [P, H2], f32)
        b1_sb = sb("b1_sb", [P, H1 // P], f32)
        h1_rows = sb("h1_rows", [P, H1], f32)
        dense_sb = h1_rows[:].rearrange("p (t d) -> p t d", t=TILES)
        h1 = sb("h1", [P, H1 // P, P], f32)
        h2 = sb("h2", [P, 2, H2], f32)
        y_cols = sb("y_cols", [P, TILES], f32)

        ring = [psum(f"ring{n}", [P, 512]) for n in range(2)]
        gram = psum("gram", [P, 2, GROUPS, P])
        banks = psum("banks", [P, 2, 512])
        h1_ps = [banks[:, 0, 0:H1 // 2], banks[:, 1, 0:H1 // 2]]
        h2_ps = [banks[:, 0 if t == TILES - 1 else 1, H1 // 2:H1 // 2 + H2] for t in range(TILES)]

        ids_landed = sem("ids_landed")
        ids_wide_landed = [sem(f"ids_wide_landed{n}") for n in range(2)]
        row_no_landed = sem("row_no_landed")
        dense_landed = sem("dense_landed")
        stage_landed = [sem(f"stage_landed{n}") for n in range(STAGE_RING)]
        mask_landed = sem("mask_landed")
        mlp_landed = sem("mlp_landed")
        rows_landed = [[sem(f"rows_landed{t}_{q}") for q in range(TURNS)] for t in range(TILES)]
        out_written = sem("out_written")

        zeros_ready = sem("zeros_ready")
        cleared = sem("cleared")
        minus_ready = sem("minus_ready")
        hi_ready = sem("hi_ready")
        lo_ready = sem("lo_ready")
        onehot_ready = sem("onehot_ready")
        distance_ready = sem("distance_ready")
        scalar_onehot_ready = sem("scalar_onehot_ready")
        wd_ready = sem("wd_ready")
        ring_filled = sem("ring_filled")
        blocks_used = sem("blocks_used")
        ids_copied = sem("ids_copied")
        drained = {"scalar": sem("drained_scalar"), "vector": sem("drained_vector")}
        dense_copied = sem("dense_copied")
        dense_lo_ready = sem("dense_lo_ready")
        gram_filled = sem("gram_filled")
        pairs_scalar = sem("pairs_scalar")
        pairs_vector = sem("pairs_vector")
        pairs_merged = sem("pairs_merged")
        pairs_hi_ready = sem("pairs_hi_ready")
        pairs_lo_ready = sem("pairs_lo_ready")
        h1_filled = sem("h1_filled")
        h1_copied = sem("h1_copied")
        h2_filled = sem("h2_filled")
        h2_read = sem("h2_read")
        y_ready = sem("y_ready")

        block = ctx.enter_context(nc.Block())

        def tile(t):
            return slice(t * P, (t + 1) * P)

        def turned(q):
            return range(q * TURN, min((q + 1) * TURN, N_GATHERED))

        def drain_target(step):
            if step[0] == "dense":
                return eT[:, :, 0]
            if step[0] == "onehot":
                return eT[:, :, 1 + step[1]]
            _, t, q = step
            slot = 1 + N_ONEHOT + q * TURN
            n = len(turned(q))
            return eT[:, tile(t), slot:slot + n].rearrange("p b f -> p f b")

        def drain_source(step):
            bank = ring[RING.index(step) % 2]
            if step[0] == "turn":
                n = len(turned(step[2]))
                return bank[:, 0:n * P].rearrange("p (f b) -> p f b", f=n)
            return bank[:, 0:BATCH]

        def groups(c):
            return slice(c * GROUPS, (c + 1) * GROUPS)

        def pairs_parts(c, s, j):
            n = packed_in(j)
            block = gram[SLOTS * s:SLOTS * s + FEATURES, c % 2, :, s * FEATURES + j:s * FEATURES + j + SPAN + QUADS * (n - 1) + 1]
            src = bass.AP(tensor=block.tensor, offset=block.offset,
                          ap=[block.ap[0], [SPAN, 2], [QUADS, n], [P, GROUPS]])
            return pairs[SLOTS * j:SLOTS * j + FEATURES, :, 0:n, s, groups(c)], src

        def chunk_of(part, c):
            return part[:, :, :, groups(c)]

        def stage_parts(n):
            slot = n % SPLIT_RING
            stage = n % STAGE_RING
            if n < N_ONEHOT:
                return (staged[:, stage].rearrange("p (k d) -> p k d", d=D), table_hi[:, slot], table_lo[:, slot])
            if n == STAGES - 1:
                return wd[:], w1_hi[:, K_TILES], w1_lo[:, K_TILES]
            k = slice((n - N_ONEHOT) * (WIDE // H1), min((n - N_ONEHOT + 1) * (WIDE // H1), K_TILES))
            size = k.stop - k.start
            return (staged[:, stage, 0:size * H1].rearrange("p (k m) -> p k m", m=H1), w1_hi[:, k], w1_lo[:, k])

        def stage_source(n):
            if n < N_ONEHOT:
                return onehot_tables[n]
            if n == STAGES - 1:
                return w1_dense
            at = (n - N_ONEHOT) * WIDE
            return w1_pairs[:, at:min(at + WIDE, K_TILES * H1)]

        def load_stage(queue, n):
            source = stage_source(n)
            queue.dma_start(staged[:, n % STAGE_RING, 0:source.shape[1]], source).then_inc(stage_landed[n % STAGE_RING], 16)

        @block.sync
        def _(sp):
            def load_ids(i):
                sp.dma_start(ids_wide[:, i % 2], ids_rows[i:i + 1].to_broadcast((P, BATCH))).then_inc(ids_wide_landed[i % 2], 16)

            sp.dma_start(ids_sb[:], ids.rearrange("(t p) f -> p t f", p=P)).then_inc(ids_landed, 16)
            load_ids(0)
            load_ids(1)
            load_stage(sp, 1)
            sp.dma_start(ident[:], identity).then_inc(dense_landed, 16)
            sp.dma_start(dense_sb, dense.rearrange("(t p) d -> p t d", p=P)).then_inc(dense_landed, 16)
            for n in range(2, STAGES):
                if n >= STAGE_RING:
                    sp.wait_ge(lo_ready, n - STAGE_RING + 1)
                load_stage(sp, n)
                if n < N_ONEHOT:
                    sp.wait_ge(ids_copied, n - 1)
                    load_ids(n)
            sp.dma_start(b_mask[:], packed_from_b).then_inc(mask_landed, 16)
            sp.dma_start(w2_sb[:], w2).then_inc(mlp_landed, 16)
            sp.dma_start(w3_bc[:], w3.to_broadcast((P, H2))).then_inc(mlp_landed, 16)
            sp.dma_start(b1_sb[:], b1).then_inc(mlp_landed, 16)
            sp.dma_start(b2_bc[:], b2.to_broadcast((P, H2))).then_inc(mlp_landed, 16)
            sp.wait_ge(y_ready, TILES)
            sp.dma_start(out, y_cols[:]).then_inc(out_written, 16)
            sp.wait_ge(out_written, 16)

        @block.gpsimd
        def _(pool):
            nc.gpsimd.memset(eT[:, :, FEATURES:SLOTS], 0.0).then_inc(cleared, 1)
            pool.wait_ge(ids_landed, 16)
            for t in range(TILES):
                for g, f in enumerate(GATHERED_TABLES):
                    if t >= 2 and g % TURN == 0:
                        pool.wait_ge(ring_filled, RING.index(("turn", t - 2, g // TURN)) + 1)
                    nc.gpsimd.indirect_dma_start(
                        rows[:, t % 2, g, :], None, tables[f],
                        bass.IndirectOffsetOnAxis(ap=ids_sb[:, t, f:f + 1], axis=0),
                    ).then_inc(rows_landed[t][g // TURN], 16)
                if t == 1:
                    pool.wait_ge(dense_copied, 2)
                    nc.gpsimd.tensor_tensor(denseT_lo[:], denseT[:].rearrange("p t s g -> p t (s g)"),
                                            denseT_hi[:].bitcast(f32), ALU.subtract).then_inc(dense_lo_ready, 1)
                    n = STAGES - 1
                    pool.wait_ge(stage_landed[n % STAGE_RING], 16 * (n // STAGE_RING + 1))
                    nc.gpsimd.tensor_tensor(wd[:], staged[:, n % STAGE_RING, 0:H1], staged[:, n % STAGE_RING, H1:2 * H1],
                                            ALU.add).then_inc(wd_ready, 1)

        @block.tensor
        def _(pe):
            pe.wait_ge(zeros_ready, 1)
            for n in range(WARM_UPS):
                nc.tensor.matmul(gram[:, 0, 0:4, :], zeros[:, 0:P], zeros[:], start=True, stop=True)

            def take_bank(step):
                n = RING.index(step)
                if n >= 2:
                    pe.wait_ge(drained[drained_by(RING[n - 2])], drains(RING[n - 2]))
                return ring[n % 2]

            for step in STEPS:
                kind = step[0]
                if kind == "dense":
                    bank = take_bank(step)
                    pe.wait_ge(dense_landed, 32)
                    for t in range(TILES):
                        last = nc.tensor.transpose(bank[:, tile(t)], dense_sb[:, t, :], ident[:])
                    last.then_inc(ring_filled, 1)
                elif kind == "onehot":
                    i = step[1]
                    bank = take_bank(step)
                    for n, (part, ready) in enumerate(((table_hi, hi_ready), (table_lo, lo_ready))):
                        pe.wait_ge(ready, i + 1)
                        for k in range(ROW_BLOCKS):
                            if n == 0:
                                if k < VECTOR_BLOCKS:
                                    pe.wait_ge(onehot_ready, i * VECTOR_BLOCKS + k + 1)
                                else:
                                    pe.wait_ge(scalar_onehot_ready, i * SCALAR_BLOCKS + k - VECTOR_BLOCKS + 1)
                            last = nc.tensor.matmul(bank[:], part[:, i % SPLIT_RING, k, :], onehot[:, i % 2, k, :],
                                                    start=(k == 0 and n == 0), stop=(k == ROW_BLOCKS - 1 and n == 1))
                            if n == 1 and k < ROW_BLOCKS - 1:
                                last.then_inc(blocks_used, 1)
                    last.then_inc(ring_filled, 1)
                elif kind == "turn":
                    _, t, q = step
                    bank = take_bank(step)
                    if q == 0 and t == 0:
                        pe.wait_ge(dense_landed, 32)
                    pe.wait_ge(rows_landed[t][q], 16 * len(turned(q)))
                    for n, g in enumerate(turned(q)):
                        last = nc.tensor.transpose(bank[:, n * P:(n + 1) * P], rows[:, t % 2, g, :], ident[:])
                    last.then_inc(ring_filled, 1)
                elif kind == "gram":
                    _, t, c = step
                    if c == 0:
                        pe.wait_ge(cleared, 2)
                        for who in ("scalar", "vector"):
                            slots = [s for s in RING if s[0] in ("dense", "onehot") or s[:2] == ("turn", t)]
                            pe.wait_ge(drained[who], max(drains(s) for s in slots if drained_by(s) == who))
                    chunk = CHUNKS * t + c
                    if chunk >= 2:
                        pe.wait_ge(pairs_scalar, chunk - 1)
                        pe.wait_ge(pairs_vector, chunk - 1)
                    for g in range(GROUPS):
                        b = t * P + (c * GROUPS + g) * QUADS
                        last = nc.tensor.matmul(
                            gram[0:GRAM_ROWS, c % 2, g, 0:QUADS * FEATURES],
                            eT[:, b:b + QUADS, :].rearrange("p b f -> p (b f)")[:, 0:GRAM_ROWS],
                            eT[:, b:b + QUADS, 0:FEATURES], start=True, stop=True)
                    last.then_inc(gram_filled, 1)
                elif kind == "layer1":
                    _, t, half, part = step
                    m = slice(half * H1 // 2, (half + 1) * H1 // 2)
                    if part == "high":
                        if t == 0 and half == 0:
                            pe.wait_ge(lo_ready, STAGES)
                        elif t >= 1:
                            pe.wait_ge(h1_copied, 2 * (t - 1) + half + 1)
                            if half == 1:
                                pe.wait_ge(h2_read, t)
                        z = [denseT_hi[:, t]] + [pairs_hi[:, k].rearrange("p s g -> p (s g)") for k in range(K_TILES)]
                        w_parts = (w1_hi, w1_lo)
                        pairs_ready = pairs_hi_ready
                    else:
                        if t == 0 and half == 0:
                            pe.wait_ge(dense_lo_ready, 1)
                        z = [denseT_lo[:, t]] + [pairs_lo[:, k].rearrange("p s g -> p (s g)") for k in range(K_TILES)]
                        w_parts = (w1_hi,)
                        pairs_ready = pairs_lo_ready
                    for n, z_part in enumerate(z):
                        if half == 0 and n == 1:
                            pe.wait_ge(pairs_ready, CHUNKS * (t + 1))
                        k = (n - 1) % (K_TILES + 1)
                        for w_part in w_parts:
                            last = nc.tensor.matmul(h1_ps[half], z_part, w_part[:, k, m],
                                                    start=(part == "high" and n == 0 and w_part is w1_hi),
                                                    stop=(part == "low" and n == K_TILES))
                    if part == "low":
                        last.then_inc(h1_filled, 1)
                elif kind == "turn_h1":
                    _, t, m, n = step
                    bank = take_bank(step)
                    pe.wait_ge(h1_copied, 2 * t + m // 2 + 1)
                    for k in range(n):
                        last = nc.tensor.transpose(bank[:, tile(k)], h1_rows[:, tile(m + k)], ident[:])
                    last.then_inc(ring_filled, 1)
                elif kind == "layer2":
                    _, t, m = step
                    if t == 0 and m == 0:
                        pe.wait_ge(mlp_landed, 64)
                    for k in (m, m + 1):
                        pe.wait_ge(drained[drained_by(h1_turn(t, k))], drains(h1_turn(t, k)))
                        last = nc.tensor.matmul(h2_ps[t], h1[:, k, :], w2_sb[:, k, :], start=(k == 0), stop=(k == H1 // P - 1))
                    if m > 0:
                        last.then_inc(h2_filled, 1)

        @block.scalar
        def _(act):
            def split_high(n):
                if n == STAGES - 1:
                    act.wait_ge(wd_ready, 1)
                else:
                    act.wait_ge(stage_landed[n % STAGE_RING], 16 * (n // STAGE_RING + 1))
                if SPLIT_RING <= n < N_ONEHOT:
                    act.wait_ge(ring_filled, RING.index(("onehot", n - SPLIT_RING)) + 1)
                whole, high, _ = stage_parts(n)
                nc.scalar.activation(high, whole, ACT.Copy).then_inc(hi_ready, 1)

            def copy_ids(i):
                act.wait_ge(ids_wide_landed[i % 2], 16 * (i // 2 + 1))
                if i >= 2:
                    act.wait_ge(onehot_ready, (i - 1) * VECTOR_BLOCKS)
                    act.wait_ge(distance_ready, (i - 1) * SCALAR_BLOCKS)
                nc.scalar.activation(ids_bc[:, i % 2, :], ids_wide[:, i % 2, :], ACT.Copy).then_inc(ids_copied, 1)

            act.dma_start(row_no[:], row_numbers).then_inc(row_no_landed, 16)
            load_stage(act, 0)
            for step in STEPS:
                kind = step[0]
                if kind == "ids":
                    i = step[1]
                    if i == 0:
                        copy_ids(0)
                    split_high(i)
                    act.wait_ge(ids_copied, i + 1)
                    if i == 0:
                        act.wait_ge(minus_ready, 1)
                    for n in range(SCALAR_BLOCKS):
                        k = VECTOR_BLOCKS + n
                        if i >= 1:
                            act.wait_ge(scalar_onehot_ready, (i - 1) * SCALAR_BLOCKS + n + 1)
                        nc.scalar.activation(distance[:, n, :], ids_bc[:, i % 2, :], ACT.Abs,
                                             bias=minus_row_no[:, k:k + 1]).then_inc(distance_ready, 1)
                    if i >= 2:
                        act.wait_ge(ring_filled, RING.index(("onehot", i - 2)) + 1)
                    for n in range(SCALAR_BLOCKS):
                        act.wait_ge(distance_ready, i * SCALAR_BLOCKS + n + 1)
                        nc.scalar.activation(onehot[:, i % 2, VECTOR_BLOCKS + n, :], distance[:, n, :], ACT.Relu,
                                             bias=1.0, scale=-1.0).then_inc(scalar_onehot_ready, 1)
                    if i + 1 < N_ONEHOT:
                        copy_ids(i + 1)
                elif kind == "split_w":
                    split_high(N_ONEHOT + step[1])
                elif kind == "dense":
                    act.wait_ge(ring_filled, RING.index(step) + 1)
                    nc.scalar.activation(
                        denseT[:], drain_source(step).rearrange("p (t g s) -> p t s g", t=TILES, s=QUADS),
                        ACT.Copy).then_inc(dense_copied, 1)
                    nc.scalar.activation(drain_target(step), drain_source(step), ACT.Copy).then_inc(drained["scalar"], 1)
                    act.wait_ge(dense_copied, 1)
                    nc.scalar.activation(denseT_hi[:], denseT[:].rearrange("p t s g -> p t (s g)"),
                                         ACT.Copy).then_inc(dense_copied, 1)
                elif kind in ("onehot", "turn") and drained_by(step) == "scalar":
                    act.wait_ge(ring_filled, RING.index(step) + 1)
                    nc.scalar.activation(drain_target(step), drain_source(step), ACT.Copy).then_inc(drained["scalar"], 1)
                elif kind == "gram":
                    _, t, c = step
                    chunk = CHUNKS * t + c
                    act.wait_ge(gram_filled, chunk + 1)
                    if t >= 1 and c == 0:
                        act.wait_ge(pairs_lo_ready, CHUNKS * t)
                    if chunk == 0:
                        act.wait_ge(cleared, 2)
                    for s in range(SCALAR_QUADS):
                        for j in range(QUADS):
                            to, of = pairs_parts(c, s, j)
                            last = nc.scalar.activation(to, of, ACT.Copy)
                    last.then_inc(pairs_scalar, 1)
                elif kind == "pack":
                    _, t, c = step
                    chunk = CHUNKS * t + c
                    act.wait_ge(pairs_merged, chunk + 1)
                    if t >= 1 and c == 0:
                        act.wait_ge(h1_filled, 2 * t)
                    nc.scalar.activation(chunk_of(pairs_hi, c), chunk_of(pairs[:, A], c), ACT.Copy).then_inc(pairs_hi_ready, 1)
                elif kind == "turn_h1" and drained_by(step) == "scalar":
                    _, t, m, n = step
                    if t == 0:
                        act.wait_ge(mlp_landed, 64)
                    else:
                        act.wait_ge(h2_filled, t)
                    act.wait_ge(ring_filled, RING.index(step) + 1)
                    for k in range(n):
                        last = nc.scalar.activation(h1[:, m + k, :], ring[RING.index(step) % 2][:, tile(k)], ACT.Relu,
                                                    bias=b1_sb[:, m + k:m + k + 1])
                    last.then_inc(drained["scalar"], 1)

        @block.vector
        def _(dve):
            nc.vector.memset(zeros[:], 0.0).then_inc(zeros_ready, 1)
            nc.vector.memset(pairs[:], 0.0).then_inc(cleared, 1)
            dve.wait_ge(row_no_landed, 16)
            nc.vector.tensor_scalar(minus_row_no[:], row_no[:], -1.0, None, ALU.mult).then_inc(minus_ready, 1)
            def split_low(n):
                dve.wait_ge(hi_ready, n + 1)
                if SPLIT_RING <= n < N_ONEHOT:
                    dve.wait_ge(ring_filled, RING.index(("onehot", n - SPLIT_RING)) + 1)
                whole, high, low = stage_parts(n)
                nc.vector.tensor_tensor(low, whole, high.bitcast(f32), ALU.subtract).then_inc(lo_ready, 1)

            def pack_low(t, c):
                dve.wait_ge(pairs_hi_ready, CHUNKS * t + c + 1)
                if t >= 1 and c == 0:
                    dve.wait_ge(h1_filled, 2 * t)
                nc.vector.tensor_tensor(chunk_of(pairs_lo, c), chunk_of(pairs[:, A], c), chunk_of(pairs_hi, c).bitcast(f32),
                                        ALU.subtract).then_inc(pairs_lo_ready, 1)

            for step in STEPS:
                kind = step[0]
                if kind == "ids":
                    i = step[1]
                    dve.wait_ge(ids_copied, i + 1)
                    for k in range(VECTOR_BLOCKS):
                        if i >= 2:
                            dve.wait_ge(blocks_used, (i - 2) * (ROW_BLOCKS - 1) + k + 1)
                        nc.vector.tensor_scalar(onehot[:, i % 2, k, :], ids_bc[:, i % 2, :], row_no[:, k:k + 1], None,
                                                ALU.is_equal).then_inc(onehot_ready, 1)
                    split_low(i)
                elif kind == "split_w":
                    split_low(N_ONEHOT + step[1])
                elif kind == "turn" and drained_by(step) == "vector":
                    dve.wait_ge(ring_filled, RING.index(step) + 1)
                    nc.vector.tensor_copy(drain_target(step), drain_source(step)).then_inc(drained["vector"], 1)
                elif kind == "gram":
                    _, t, c = step
                    chunk = CHUNKS * t + c
                    dve.wait_ge(gram_filled, chunk + 1)
                    if t >= 1 and c == 0:
                        dve.wait_ge(pairs_lo_ready, CHUNKS * t)
                    if chunk == 0:
                        dve.wait_ge(cleared, 2)
                    for s in range(SCALAR_QUADS, QUADS):
                        for j in range(QUADS):
                            to, of = pairs_parts(c, s, j)
                            last = nc.vector.tensor_copy(to, of)
                    last.then_inc(pairs_vector, 1)
                elif kind == "pack":
                    _, t, c = step
                    chunk = CHUNKS * t + c
                    if chunk == 0:
                        dve.wait_ge(mask_landed, 16)
                    dve.wait_ge(pairs_scalar, chunk + 1)
                    dve.wait_ge(pairs_vector, chunk + 1)
                    nc.vector.copy_predicated(chunk_of(pairs[:, A], c), b_mask[:].rearrange("p k (s g) -> p k s g", s=QUADS),
                                              chunk_of(pairs[:, B], c)).then_inc(pairs_merged, 1)
                    if c >= 1:
                        pack_low(t, c - 1)
                    if c == CHUNKS - 1:
                        pack_low(t, c)
                elif kind == "layer1":
                    _, t, half, part = step
                    if part == "high":
                        continue
                    dve.wait_ge(h1_filled, 2 * t + half + 1)
                    if t >= 1:
                        dve.wait_ge(ring_filled, RING.index(h1_turn(t - 1, 2 * half + 1)) + 1)
                    nc.vector.tensor_copy(h1_rows[:, half * H1 // 2:(half + 1) * H1 // 2], h1_ps[half]).then_inc(h1_copied, 1)
                elif kind == "turn_h1" and drained_by(step) == "vector":
                    _, t, m, n = step
                    if t == 0:
                        dve.wait_ge(mlp_landed, 64)
                    else:
                        dve.wait_ge(h2_filled, t)
                    dve.wait_ge(ring_filled, RING.index(step) + 1)
                    for k in range(n):
                        last = nc.vector.tensor_scalar(h1[:, m + k, :], ring[RING.index(step) % 2][:, tile(k)],
                                                       b1_sb[:, m + k:m + k + 1], 0.0, ALU.add, ALU.max)
                    last.then_inc(drained["vector"], 1)
                elif kind == "layer2" and step[2] > 0:
                    t = step[1]
                    dve.wait_ge(h2_filled, t + 1)
                    if t >= 1:
                        dve.wait_ge(y_ready, t)
                    nc.vector.tensor_tensor(h2[:, 0, :], h2_ps[t], b2_bc[:], ALU.add).then_inc(h2_read, 1)
                    dve.wait_ge(h2_read, t + 1)
                    nc.vector.scalar_tensor_tensor(h2[:, 1, :], h2[:, 0, :], 0.0, w3_bc[:], ALU.max, ALU.mult,
                                                   accum_out=y_cols[:, t:t + 1]).then_inc(y_ready, 1)


def layouts(inputs):
    import numpy as np

    def array(name):
        return np.ascontiguousarray(inputs[name])

    w1 = array("W_top1")
    w1_pairs = np.zeros((QUADS, SLOTS, K_TILES, H1), w1.dtype)
    feature = [0] + [1 + f for f in SLOT_TABLE]
    first = {}
    row = D
    for f in range(FEATURES):
        for g in range(f + 1, FEATURES):
            first[f, g] = row
            row += 1
    mask = np.zeros((QUADS, SLOTS, K_TILES), np.int32)
    for i in range(PACKED):
        for r in range(FEATURES):
            at = i % QUADS, r, i // QUADS
            mask[at] = from_b(i, r)
            if packed_pair(i, r):
                w1_pairs[at] = w1[first[tuple(sorted(feature[slot] for slot in packed_pair(i, r)))]]
    onehot_tables = np.zeros((N_ONEHOT, TABLE_ROWS, D), w1.dtype)
    for i, f in enumerate(ONEHOT_TABLES):
        table = array(f"tbl_{f}")
        onehot_tables[i, :len(table)] = table
    ids = array("ids")
    out = {
        "dense": array("r_dense_features"),
        "ids": ids,
        "ids_rows": np.ascontiguousarray(ids.T[list(ONEHOT_TABLES)]),
        "onehot_tables": onehot_tables.reshape(N_ONEHOT, P, WIDE),
        "w1_dense": np.concatenate([w1[:D], w1[row:row + D]], axis=1),
        "w1_pairs": w1_pairs.reshape(P, K_TILES * H1),
        "w2": np.ascontiguousarray(array("W_top2").reshape(H1 // P, P, H2).transpose(1, 0, 2)),
        "w3": array("W_top3").reshape(1, H2),
        "b1": np.ascontiguousarray(array("b_top1").reshape(H1 // P, P).T),
        "b2": array("b_top2").reshape(1, H2),
        "identity": np.eye(P, dtype=np.float32),
        "row_numbers": np.arange(TABLE_ROWS, dtype=np.float32).reshape(P, ROW_BLOCKS),
        "packed_from_b": np.repeat(mask.reshape(P, K_TILES, 1), P // CHUNKS, axis=2),
    }
    for f in GATHERED_TABLES:
        out[f"tbl_{f}"] = array(f"tbl_{f}")
    return out


def kernel(**inputs):
    import numpy as np
    import concourse.bacc as bacc
    from concourse.bass_utils import run_bass_kernel_spmd

    nc = bacc.Bacc("TRN2", target_bir_lowering=False, num_devices=1)
    arrays, aps = {}, {}
    for name, a in layouts(inputs).items():
        arrays[f"in_{name}"] = a
        aps[name] = nc.dram_tensor(f"in_{name}", a.shape, mybir.dt.from_np(a.dtype), kind="ExternalInput").ap()
    out = nc.dram_tensor("out", (P, TILES), mybir.dt.float32, kind="ExternalOutput").ap()
    tables = {f: aps.pop(f"tbl_{f}") for f in GATHERED_TABLES}
    dlrm_tower(nc, tables=tables, out=out, **aps)
    result = run_bass_kernel_spmd(nc, [arrays], core_ids=[0])
    y = result.results[0]["out"].reshape(QUADS, P // QUADS, TILES)
    return y.transpose(2, 1, 0).reshape(BATCH, 1)
```
